# Optimizing a Trainium2 kernel written in Bass

```python
import numpy as np
import jax
import jax.numpy as jnp

def _softmax(x, axis=-1):
    return jax.nn.softmax(x, axis=axis)

def _gelu(x):
    return jax.nn.gelu(x, approximate=True)

def _silu(x):
    return jax.nn.silu(x)

def _sigmoid(x):
    return jax.nn.sigmoid(x)

def _layernorm(x, axis=-1, eps=1e-05):
    m = jnp.mean(x, axis=axis, keepdims=True)
    v = jnp.var(x, axis=axis, keepdims=True)
    return (x - m) / jnp.sqrt(v + eps)

def _scatter_add(tgt, idx, src, axis=0):
    return tgt.at[idx].add(src)

def _segment_sum(src, seg, n):
    return jax.ops.segment_sum(src, seg, n)
kernel_name = 'mk_dlrm_tower_d1_rec_r8_8ffcb0'

def setup_inputs(seed: int=0):
    np.random.seed(seed)
    _w = jnp.asarray

    def _rec_inputs():
        import jax
        import jax.numpy as jnp
        _tk = jax.random.key(seed)
        dense_ctx = jax.random.normal(jax.random.fold_in(_tk, 190), (512, 16), jnp.float32)
        ids = jnp.stack([jax.random.randint(jax.random.fold_in(_tk, 200 + f), (512,), 0, v, jnp.int32) for f, v in enumerate([1250, 1250, 125000, 1250, 1250, 125000, 12500, 1000, 1250, 1250, 1000, 125000, 125000, 12500, 12500, 125000, 1000, 1250, 12500, 1250, 1250, 1000, 1250, 12500, 1000, 1250, 125000, 1000, 1250, 12500, 125000, 125000, 1250, 1250, 1000, 125000, 125000, 125000, 125000, 1250])], axis=1)
        tbl_0 = 0.05 * jax.random.normal(jax.random.fold_in(_tk, 500 + 0), (1250, 16), jnp.float32)
        tbl_1 = 0.05 * jax.random.normal(jax.random.fold_in(_tk, 500 + 1), (1250, 16), jnp.float32)
        tbl_2 = 0.05 * jax.random.normal(jax.random.fold_in(_tk, 500 + 2), (125000, 16), jnp.float32)
        tbl_3 = 0.05 * jax.random.normal(jax.random.fold_in(_tk, 500 + 3), (1250, 16), jnp.float32)
        tbl_4 = 0.05 * jax.random.normal(jax.random.fold_in(_tk, 500 + 4), (1250, 16), jnp.float32)
        tbl_5 = 0.05 * jax.random.normal(jax.random.fold_in(_tk, 500 + 5), (125000, 16), jnp.float32)
        tbl_6 = 0.05 * jax.random.normal(jax.random.fold_in(_tk, 500 + 6), (12500, 16), jnp.float32)
        tbl_7 = 0.05 * jax.random.normal(jax.random.fold_in(_tk, 500 + 7), (1000, 16), jnp.float32)
        tbl_8 = 0.05 * jax.random.normal(jax.random.fold_in(_tk, 500 + 8), (1250, 16), jnp.float32)
        tbl_9 = 0.05 * jax.random.normal(jax.random.fold_in(_tk, 500 + 9), (1250, 16), jnp.float32)
        tbl_10 = 0.05 * jax.random.normal(jax.random.fold_in(_tk, 500 + 10), (1000, 16), jnp.float32)
        tbl_11 = 0.05 * jax.random.normal(jax.random.fold_in(_tk, 500 + 11), (125000, 16), jnp.float32)
        tbl_12 = 0.05 * jax.random.normal(jax.random.fold_in(_tk, 500 + 12), (125000, 16), jnp.float32)
        tbl_13 = 0.05 * jax.random.normal(jax.random.fold_in(_tk, 500 + 13), (12500, 16), jnp.float32)
        tbl_14 = 0.05 * jax.random.normal(jax.random.fold_in(_tk, 500 + 14), (12500, 16), jnp.float32)
        tbl_15 = 0.05 * jax.random.normal(jax.random.fold_in(_tk, 500 + 15), (125000, 16), jnp.float32)
        tbl_16 = 0.05 * jax.random.normal(jax.random.fold_in(_tk, 500 + 16), (1000, 16), jnp.float32)
        tbl_17 = 0.05 * jax.random.normal(jax.random.fold_in(_tk, 500 + 17), (1250, 16), jnp.float32)
        tbl_18 = 0.05 * jax.random.normal(jax.random.fold_in(_tk, 500 + 18), (12500, 16), jnp.float32)
        tbl_19 = 0.05 * jax.random.normal(jax.random.fold_in(_tk, 500 + 19), (1250, 16), jnp.float32)
        tbl_20 = 0.05 * jax.random.normal(jax.random.fold_in(_tk, 500 + 20), (1250, 16), jnp.float32)
        tbl_21 = 0.05 * jax.random.normal(jax.random.fold_in(_tk, 500 + 21), (1000, 16), jnp.float32)
        tbl_22 = 0.05 * jax.random.normal(jax.random.fold_in(_tk, 500 + 22), (1250, 16), jnp.float32)
        tbl_23 = 0.05 * jax.random.normal(jax.random.fold_in(_tk, 500 + 23), (12500, 16), jnp.float32)
        tbl_24 = 0.05 * jax.random.normal(jax.random.fold_in(_tk, 500 + 24), (1000, 16), jnp.float32)
        tbl_25 = 0.05 * jax.random.normal(jax.random.fold_in(_tk, 500 + 25), (1250, 16), jnp.float32)
        tbl_26 = 0.05 * jax.random.normal(jax.random.fold_in(_tk, 500 + 26), (125000, 16), jnp.float32)
        tbl_27 = 0.05 * jax.random.normal(jax.random.fold_in(_tk, 500 + 27), (1000, 16), jnp.float32)
        tbl_28 = 0.05 * jax.random.normal(jax.random.fold_in(_tk, 500 + 28), (1250, 16), jnp.float32)
        tbl_29 = 0.05 * jax.random.normal(jax.random.fold_in(_tk, 500 + 29), (12500, 16), jnp.float32)
        tbl_30 = 0.05 * jax.random.normal(jax.random.fold_in(_tk, 500 + 30), (125000, 16), jnp.float32)
        tbl_31 = 0.05 * jax.random.normal(jax.random.fold_in(_tk, 500 + 31), (125000, 16), jnp.float32)
        tbl_32 = 0.05 * jax.random.normal(jax.random.fold_in(_tk, 500 + 32), (1250, 16), jnp.float32)
        tbl_33 = 0.05 * jax.random.normal(jax.random.fold_in(_tk, 500 + 33), (1250, 16), jnp.float32)
        tbl_34 = 0.05 * jax.random.normal(jax.random.fold_in(_tk, 500 + 34), (1000, 16), jnp.float32)
        tbl_35 = 0.05 * jax.random.normal(jax.random.fold_in(_tk, 500 + 35), (125000, 16), jnp.float32)
        tbl_36 = 0.05 * jax.random.normal(jax.random.fold_in(_tk, 500 + 36), (125000, 16), jnp.float32)
        tbl_37 = 0.05 * jax.random.normal(jax.random.fold_in(_tk, 500 + 37), (125000, 16), jnp.float32)
        tbl_38 = 0.05 * jax.random.normal(jax.random.fold_in(_tk, 500 + 38), (125000, 16), jnp.float32)
        tbl_39 = 0.05 * jax.random.normal(jax.random.fold_in(_tk, 500 + 39), (1250, 16), jnp.float32)
        _rk = jax.random.fold_in(_tk, 7)
        W_top1 = 0.05 * jax.random.normal(jax.random.fold_in(_tk, 801), (400, 512), jnp.float32)
        W_top2 = 0.0441942 * jax.random.normal(jax.random.fold_in(_tk, 802), (512, 256), jnp.float32)
        W_top3 = 0.0625 * jax.random.normal(jax.random.fold_in(_tk, 803), (256, 1), jnp.float32)
        b_top1 = jnp.zeros((512,), jnp.float32)
        b_top2 = jnp.zeros((256,), jnp.float32)
        return (dense_ctx, ids, tbl_0, tbl_1, tbl_2, tbl_3, tbl_4, tbl_5, tbl_6, tbl_7, tbl_8, tbl_9, tbl_10, tbl_11, tbl_12, tbl_13, tbl_14, tbl_15, tbl_16, tbl_17, tbl_18, tbl_19, tbl_20, tbl_21, tbl_22, tbl_23, tbl_24, tbl_25, tbl_26, tbl_27, tbl_28, tbl_29, tbl_30, tbl_31, tbl_32, tbl_33, tbl_34, tbl_35, tbl_36, tbl_37, tbl_38, tbl_39, W_top1, b_top1, W_top2, b_top2, W_top3)
    dense_ctx, ids, tbl_0, tbl_1, tbl_2, tbl_3, tbl_4, tbl_5, tbl_6, tbl_7, tbl_8, tbl_9, tbl_10, tbl_11, tbl_12, tbl_13, tbl_14, tbl_15, tbl_16, tbl_17, tbl_18, tbl_19, tbl_20, tbl_21, tbl_22, tbl_23, tbl_24, tbl_25, tbl_26, tbl_27, tbl_28, tbl_29, tbl_30, tbl_31, tbl_32, tbl_33, tbl_34, tbl_35, tbl_36, tbl_37, tbl_38, tbl_39, W_top1, b_top1, W_top2, b_top2, W_top3 = _rec_inputs()

    def _L0_rec_setup():
        import jax, jax.numpy as jnp
        import numpy as np
        B, M, D = (512, 40, 16)
        DIMS = [128, 128, 128]
        key = jax.random.key(seed)
        k_x, k0, k1, k2 = jax.random.split(key, 4)
        scale = lambda fan_in: (2.0 / fan_in) ** 0.5
        x0 = jax.random.normal(k_x, (B, M, D), dtype=jnp.float32)
        kern0 = jax.random.normal(k0, (DIMS[0], M, M), dtype=jnp.float32) * scale(M * M)
        kern1 = jax.random.normal(k1, (DIMS[1], DIMS[0], M), dtype=jnp.float32) * scale(DIMS[0] * M)
        kern2 = jax.random.normal(k2, (DIMS[2], DIMS[1], M), dtype=jnp.float32) * scale(DIMS[1] * M)
        return {'x0': x0, 'k0': kern0, 'k1': kern1, 'k2': kern2}
    _L0_rec_all = _L0_rec_setup()
    _L0_rec_in = {k: v for k, v in _L0_rec_all.items() if k in ('k0', 'k1', 'k2')}
    del _L0_rec_all
    return {'dense_ctx': dense_ctx, 'ids': ids, 'tbl_0': tbl_0, 'tbl_1': tbl_1, 'tbl_2': tbl_2, 'tbl_3': tbl_3, 'tbl_4': tbl_4, 'tbl_5': tbl_5, 'tbl_6': tbl_6, 'tbl_7': tbl_7, 'tbl_8': tbl_8, 'tbl_9': tbl_9, 'tbl_10': tbl_10, 'tbl_11': tbl_11, 'tbl_12': tbl_12, 'tbl_13': tbl_13, 'tbl_14': tbl_14, 'tbl_15': tbl_15, 'tbl_16': tbl_16, 'tbl_17': tbl_17, 'tbl_18': tbl_18, 'tbl_19': tbl_19, 'tbl_20': tbl_20, 'tbl_21': tbl_21, 'tbl_22': tbl_22, 'tbl_23': tbl_23, 'tbl_24': tbl_24, 'tbl_25': tbl_25, 'tbl_26': tbl_26, 'tbl_27': tbl_27, 'tbl_28': tbl_28, 'tbl_29': tbl_29, 'tbl_30': tbl_30, 'tbl_31': tbl_31, 'tbl_32': tbl_32, 'tbl_33': tbl_33, 'tbl_34': tbl_34, 'tbl_35': tbl_35, 'tbl_36': tbl_36, 'tbl_37': tbl_37, 'tbl_38': tbl_38, 'tbl_39': tbl_39, 'W_top1': W_top1, 'b_top1': b_top1, 'W_top2': W_top2, 'b_top2': b_top2, 'W_top3': W_top3, 'L0_rec_k0': _L0_rec_in['k0'], 'L0_rec_k1': _L0_rec_in['k1'], 'L0_rec_k2': _L0_rec_in['k2']}

def reference(dense_ctx, ids, tbl_0, tbl_1, tbl_2, tbl_3, tbl_4, tbl_5, tbl_6, tbl_7, tbl_8, tbl_9, tbl_10, tbl_11, tbl_12, tbl_13, tbl_14, tbl_15, tbl_16, tbl_17, tbl_18, tbl_19, tbl_20, tbl_21, tbl_22, tbl_23, tbl_24, tbl_25, tbl_26, tbl_27, tbl_28, tbl_29, tbl_30, tbl_31, tbl_32, tbl_33, tbl_34, tbl_35, tbl_36, tbl_37, tbl_38, tbl_39, W_top1, b_top1, W_top2, b_top2, W_top3, L0_rec_k0, L0_rec_k1, L0_rec_k2):
    import jax
    import jax.numpy as jnp

    def _L0_rec_ref(x0, k0, k1, k2):
        import jax, jax.numpy as jnp
        import numpy as np
        B, M, D = (512, 40, 16)
        DIMS = [128, 128, 128]
        x = x0
        outputs = []
        for k in (k0, k1, k2):
            x = jnp.einsum('bhd,bmd,ohm->bod', x, x0, k)
            outputs.append(jnp.sum(x, axis=-1))
        return jnp.concatenate(outputs, axis=1)
    e = jnp.stack([tbl_0[ids[:, 0]], tbl_1[ids[:, 1]], tbl_2[ids[:, 2]], tbl_3[ids[:, 3]], tbl_4[ids[:, 4]], tbl_5[ids[:, 5]], tbl_6[ids[:, 6]], tbl_7[ids[:, 7]], tbl_8[ids[:, 8]], tbl_9[ids[:, 9]], tbl_10[ids[:, 10]], tbl_11[ids[:, 11]], tbl_12[ids[:, 12]], tbl_13[ids[:, 13]], tbl_14[ids[:, 14]], tbl_15[ids[:, 15]], tbl_16[ids[:, 16]], tbl_17[ids[:, 17]], tbl_18[ids[:, 18]], tbl_19[ids[:, 19]], tbl_20[ids[:, 20]], tbl_21[ids[:, 21]], tbl_22[ids[:, 22]], tbl_23[ids[:, 23]], tbl_24[ids[:, 24]], tbl_25[ids[:, 25]], tbl_26[ids[:, 26]], tbl_27[ids[:, 27]], tbl_28[ids[:, 28]], tbl_29[ids[:, 29]], tbl_30[ids[:, 30]], tbl_31[ids[:, 31]], tbl_32[ids[:, 32]], tbl_33[ids[:, 33]], tbl_34[ids[:, 34]], tbl_35[ids[:, 35]], tbl_36[ids[:, 36]], tbl_37[ids[:, 37]], tbl_38[ids[:, 38]], tbl_39[ids[:, 39]]], axis=1)
    z = _L0_rec_ref(e, L0_rec_k0, L0_rec_k1, L0_rec_k2)
    z = z.reshape(z.shape[0], -1)
    h = jnp.concatenate([z, dense_ctx], axis=1)
    h = jnp.maximum(h @ W_top1 + b_top1, 0.0)
    h = jnp.maximum(h @ W_top2 + b_top2, 0.0)
    y = h @ W_top3
    return y

_drawn_inputs = setup_inputs


def setup_inputs(seed=0):
    import zlib

    import numpy as np

    out = dict(_drawn_inputs(seed))
    spreads = {'b_top1': (0.0, 0.53), 'b_top2': (0.0, 0.1)}
    factors = {'tbl_0': 7.637,
     'tbl_1': 7.149,
     'tbl_2': 6.631,
     'tbl_3': 6.974,
     'tbl_4': 7.064,
     'tbl_5': 6.766,
     'tbl_6': 6.926,
     'tbl_7': 7.507,
     'tbl_8': 6.827,
     'tbl_9': 7.111,
     'tbl_10': 6.865,
     'tbl_11': 6.913,
     'tbl_12': 6.823,
     'tbl_13': 7.267,
     'tbl_14': 7.121,
     'tbl_15': 6.873,
     'tbl_16': 6.952,
     'tbl_17': 5.762,
     'tbl_18': 7.304,
     'tbl_19': 6.771,
     'tbl_20': 6.817,
     'tbl_21': 7.85,
     'tbl_22': 7.094,
     'tbl_23': 6.819,
     'tbl_24': 7.214,
     'tbl_25': 6.967,
     'tbl_26': 6.622,
     'tbl_27': 6.977,
     'tbl_28': 6.646,
     'tbl_29': 7.292,
     'tbl_30': 6.847,
     'tbl_31': 7.154,
     'tbl_32': 6.984,
     'tbl_33': 6.174,
     'tbl_34': 7.304,
     'tbl_35': 6.509,
     'tbl_36': 7.124,
     'tbl_37': 6.321,
     'tbl_38': 7.242,
     'tbl_39': 6.739,
     'L0_rec_k1': 8.0,
     'L0_rec_k2': 8.0}
    for name, (base, spread) in spreads.items():
        noise = np.random.default_rng([zlib.crc32(name.encode()), seed]).standard_normal(out[name].shape)
        drawn = base * np.exp(spread * noise) if base else spread * noise
        out[name] = jnp.asarray(drawn.astype(out[name].dtype))
    for name, factor in factors.items():
        out[name] = (out[name] * factor).astype(out[name].dtype)
    return out
```

```python
import concourse.bass as bass
from concourse import mybir
from contextlib import ExitStack

B, M, D, O = 512, 40, 16, 128
P = 128
BT = B // P
GROUP = 512
GPB = P * D // GROUP
TPG = GROUP // P
SB = P // D
NTILES = B * D // P
MT = 65
MH = M + 1
KD = M // 2 + 1
KC = 3
NC0 = KD // KC
PR = KC * M
LO = 64
XR = LO + M
BANK = 512
MB = BANK // O
NCH = M // MB
YB = 4
OWNER = "ADDADADDAD"
NA, ND = OWNER.count("A"), OWNER.count("D")
STT = ND * MB
CTX = 16
H1, H2 = 512, 256

AT = {"a3": 8, "xtok": 11, "x1": 35}
AT.update({f"xt{q}": 2 * q for q in range(4)})
AT.update({f"roll{c}": 10 + 3.5 * c // 1 for c in range(NC0)})
AT.update({f"l0_{c}": 13 + 3.5 * c // 1 for c in range(NC0)})
FINISH_AT, G_AT = 2, 6


def rank(c):
    return OWNER[:c + 1].count(OWNER[c])


def prep_steps(with_xt):
    names = [f"xt{q}" for q in range(4)] * with_xt + ["a3", "xtok"]
    names += [f"roll{c}" for c in range(NC0)] + [f"l0_{c}" for c in range(NC0)] + ["x1"]
    return sorted(names, key=lambda n: AT[n])


def g_odd(slot):
    return (slot + 1) % 2


def empties(step):
    if step in ("a3", "xtok"):
        return "A"
    return "D" if step[:2] == "xt" or step[:4] == "roll" else None


def sel_use(u, slot, step):
    uses = [n for n in prep_steps(slot in (-1, GPB - 1)) if empties(n)]
    i = uses.index(step)
    g = u * GPB + slot + 1 if slot >= 0 else 0
    xts = 4 * (u + 1) if slot >= 0 else 0
    base = {"A": 2 * g, "D": xts + NC0 * g}
    count = {w: base[w] + sum(empties(n) == w for n in uses[:i + 1]) for w in "AD"}
    bank = (slot + 1 + i) % 2
    if i >= 2:
        w = empties(uses[i - 2])
        former = (w, base[w] + sum(empties(n) == w for n in uses[:i - 1]))
    else:
        former = ("D", base["D"] - 1 + i) if slot >= 0 else None
    return bank, xts + 9 * g + i + 1, count, former


def build(nc, ids, tables, k0a, k0b, k1, k2, ctxT, w1, w1c, b1, w2, b2, w3, selw_in, ident_in, mask_in, out):
    f32, f32r, i32 = mybir.dt.float32, mybir.dt.float32r, mybir.dt.int32
    ALU = mybir.AluOpType
    ACT = mybir.ActivationFunctionType
    AX = mybir.AxisListType
    ctx = ExitStack()
    with ctx:
        def sb(name, shape, dt=f32):
            return ctx.enter_context(nc.sbuf_tensor(name, shape, dt))

        def bank(name):
            return ctx.enter_context(nc.psum_tensor(name, [P, BANK], f32))

        def sem(name):
            return ctx.enter_context(nc.semaphore(name))

        idx = sb("idx", [P, BT, M], i32)
        idx_now = sb("idx_now", [P, M], i32)
        x0g = sb("x0g", [P, MT, D])
        XT = sb("XT", [XR, P * D], f32r)
        A3 = sb("A3", [P, GROUP])
        prod = [sb(f"prod{i}", [P, GROUP]) for i in range(2)]
        x1hi = [sb(f"x1hi{i}", [P, GROUP], f32r) for i in range(2)]
        x1lo = [sb(f"x1lo{i}", [P, GROUP], f32r) for i in range(2)]
        xtok = [sb(f"xtok{i}", [P, TPG, M]) for i in range(2)]
        scaled = [sb(f"scaled{i}", [P, NA, BANK]) for i in range(2)]
        scaled_sum = [sb(f"scaled_sum{i}", [P, O]) for i in range(2)]
        chain = [sb(f"chain{i}", [P, 2, O]) for i in range(2)]
        chain_sum = sb("chain_sum", [P, O])
        x2 = [sb(f"x2_{i}", [P, O]) for i in range(2)]
        diag = [sb(f"diag{i}", [P, MH, SB]) for i in range(2)]
        G = sb("G", [P, MH, SB + B])
        z0 = sb("z0", [P, B])
        z2 = x0g[:, 0:B // D, :].rearrange("p m d -> p (m d)")
        w0 = sb("w0", [P, 2 * H1])
        k1hi = sb("k1hi", [P, M * O], f32r)
        k1lo = sb("k1lo", [P, M * O], f32r)
        k1raw = G[:, 0:NCH, 0:BANK]
        k2s = sb("k2s", [P, M, O])
        w0a, w0b = (G[0:PR, i:i + 2, 0:NC0 * O // 2] for i in (NCH, NCH + 2))
        selraw = G[0:XR, NCH + 4:NCH + 6, 0:(NC0 + 1) * PR // 2]
        credit = sb("credit", [1, 8])
        selw = sb("selw", [XR, (NC0 + 1) * PR], f32r)
        ident = sb("ident", [P, P])
        mask = sb("mask", [P, SB])
        w1s = [A3, *prod]
        w1cs, ctxs = w0[0:CTX, 0:H1], w0[0:CTX, H1:2 * H1]
        w2s = scaled[1][:, 2:4, :].rearrange("p a (k n) -> p (a k) n", n=H2)
        w3s = sb("w3s", [P, H2 // P])
        b1s = sb("b1s", [P, H1 // P])
        b2s = sb("b2s", [P, H2 // P])
        h1, h2 = scaled[0], scaled[1]
        ys = sb("ys", [1, B])

        Y = [bank(f"Y{i}") for i in range(YB)]
        SEL = [bank(f"SEL{i}") for i in range(2)]
        X1 = bank("X1")
        GB = bank("GB")

        s_idx, s_k1, s_const, s_w0, s_mlp, s_k2 = [sem(n) for n in (
            "idx_in", "k1_in", "const_in", "w0_in", "mlp_in", "k2_in")]
        s_gzero = sem("x0g_padded")
        s_gather, s_idxnow = sem("gathered"), sem("idx_ready")
        s_k1hi, s_k1lo, s_selw, s_w0sum, s_xtzero, s_dzero, s_dones = [sem(n) for n in (
            "k1hi_ready", "k1lo_ready", "selw_ready", "w0_ready", "xt_zeroed", "diag_zeroed", "diag_ones")]
        s_sel = sem("sel_filled")
        s_selE = {"A": sem("sel_emptied_by_act"), "D": sem("sel_emptied_by_dve")}
        s_xthi = sem("xt_high_ready")
        s_l0 = sem("l0_done")
        s_x1hi, s_x1lo, s_x1free = sem("x1_high_ready"), sem("x1_low_ready"), sem("x1_bank_free")
        s_y, s_yA = sem("y_filled"), sem("y_emptied_by_act")
        s_chain = sem("chain_steps")
        s_fold = sem("pool_folds")
        s_sum, s_csum, s_x2 = sem("scaled_sum_ready"), sem("chain_sum_ready"), sem("x2_ready")
        s_diag, s_G, s_Gout = sem("diag_ready"), sem("g_filled"), sem("g_copied")
        s_z2, s_z2s, s_h1, s_h1s, s_h2, s_h2s, s_yy, s_ys, s_out = [sem(n) for n in (
            "z2_filled", "z2_ready", "h1_filled", "h1_ready", "h2_filled", "h2_ready", "out_filled",
            "out_ready", "stored")]

        block = ctx.enter_context(nc.Block())

        def over_b_tiles(eng, body):
            with eng.Fori(0, BT - 1) as u:
                body(u, False)
            body(BT - 1, True)

        def steps_at(slot, last, p):
            if last and slot == GPB - 1:
                return []
            return [n for n in prep_steps(slot == GPB - 1) if AT[n] == p]

        def a3_ready(u, slot):
            return sel_use(u, slot, "a3")[2]["A"]

        def xtok_ready(g):
            return 2 * (g + 1)

        @block.sync
        def _(sp):
            sp.dma_start(idx[:, :, :], ids).then_inc(s_idx, 16)
            sp.dma_start(selraw, selw_in.rearrange("p (a n) -> p a n", a=2)).then_inc(s_const, 16)
            sp.dma_start(ident[:, :], ident_in).then_inc(s_const, 16)
            sp.dma_start(mask[:, :], mask_in).then_inc(s_const, 16)
            sp.dma_start(k1raw, k1.rearrange("h (c n) -> h c n", n=BANK)).then_inc(s_k1, 16)
            sp.dma_start(w0a, k0a.rearrange("p (a n) -> p a n", a=2)).then_inc(s_w0, 16)
            sp.dma_start(w0b, k0b.rearrange("p (a n) -> p a n", a=2)).then_inc(s_w0, 16)
            sp.dma_start(k2s[:, :, :], k2.rearrange("h (m o) -> h m o", o=O)).then_inc(s_k2, 16)
            sp.dma_start(w3s[:, :], w3).then_inc(s_mlp, 16)
            sp.dma_start(b1s[:, :], b1).then_inc(s_mlp, 16)
            sp.dma_start(b2s[:, :], b2).then_inc(s_mlp, 16)
            sp.wait_ge(s_x1free, BT * GPB)
            for k in range(3):
                sp.dma_start(w1s[k][:, :], w1[k * P:(k + 1) * P, :]).then_inc(s_mlp, 16)
            sp.dma_start(w1cs, w1c).then_inc(s_mlp, 16)
            sp.dma_start(ctxs, ctxT).then_inc(s_mlp, 16)
            sp.wait_ge(s_sum, NTILES + 2)
            sp.dma_start(w2s, w2.rearrange("(c p) n -> p c n", p=P)).then_inc(s_mlp, 16)
            sp.wait_ge(s_ys, 1)
            sp.dma_start(out, ys[:, :]).then_inc(s_out, 16)
            sp.wait_ge(s_out, 16)

        @block.gpsimd
        def _(pool):
            def take_ids(t):
                nc.gpsimd.tensor_copy(idx_now[:, :], idx[:, t, :]).then_inc(s_idxnow, 1)
                pool.wait_ge(s_idxnow, t + 1)

            def gather(fields):
                for m in fields:
                    nc.gpsimd.indirect_dma_start(
                        x0g[:, m, :], None, tables[m],
                        bass.IndirectOffsetOnAxis(ap=idx_now[:, m:m + 1], axis=0)).then_inc(s_gather, 16)

            pool.wait_ge(s_idx, 16)
            take_ids(0)
            gather(range(M))
            for i in range(2):
                nc.gpsimd.memset(diag[i][:, :, :], 0.0).then_inc(s_dzero, 1)
            pool.wait_ge(s_dzero, 2)
            pool.wait_ge(s_const, 48)
            for i in range(2):
                nc.gpsimd.tensor_copy(diag[i][:, M, :], mask[:, :]).then_inc(s_dones, 1)
            pool.wait_ge(s_dones, 2)
            nc.gpsimd.memset(scaled_sum[1][:, :], 0.0).then_inc(s_sum, 2)
            nc.gpsimd.memset(credit[:, 0:1], 0.0).then_inc(s_G, 1)
            nc.gpsimd.memset(credit[:, 1:2], 0.0).then_inc(s_diag, 1)

            def body(u, last):
                for tile in range(GPB * TPG):
                    slot, j = tile // TPG, tile % TPG
                    T = u * (GPB * TPG) + tile
                    pool.wait_ge(s_selE["A"], xtok_ready(u * GPB + slot))
                    pool.wait_ge(s_G, T + 1)
                    nc.gpsimd.tensor_tensor(
                        diag[tile % 2][:, 0:M, :],
                        xtok[slot % 2][:, j, :].unsqueeze(2).to_broadcast([P, M, SB]),
                        mask[:, :].unsqueeze(1).to_broadcast([P, M, SB]), ALU.mult).then_inc(s_diag, 1)
                    S = scaled[tile % 2]
                    for a in range(1, NA):
                        pool.wait_ge(s_yA, NA * (T + 1) + a + 1)
                        if a > 1:
                            pool.wait_ge(s_fold, NA * T + a - 1)
                        nc.gpsimd.tensor_tensor(S[:, 0, :], S[:, 0, :], S[:, a, :], ALU.add).then_inc(s_fold, 1)
                    pool.wait_ge(s_fold, NA * T + NA - 1)
                    nc.gpsimd.tensor_tensor(S[:, 0, 0:2 * O], S[:, 0, 0:2 * O], S[:, 0, 2 * O:4 * O],
                                            ALU.add).then_inc(s_fold, 1)
                    pool.wait_ge(s_fold, NA * T + NA)
                    pool.wait_ge(s_x2, T + 1)
                    nc.gpsimd.tensor_tensor(scaled_sum[tile % 2][:, :], S[:, 0, 0:O], S[:, 0, O:2 * O],
                                            ALU.add).then_inc(s_sum, 1)
                    if not last and tile == 0:
                        pool.wait_ge(s_xthi, 4 * (u + 1))
                        take_ids(u + 1)
                    if not last and 1 <= tile <= M // 4:
                        gather(range(4 * (tile - 1), 4 * tile))
            over_b_tiles(pool, body)

        @block.scalar
        def _(act):
            def prep(step, u, slot):
                g, par = (u * GPB + slot + 1, (slot + 1) % 2) if slot >= 0 else (0, 0)
                if empties(step):
                    bank, filled, _, _ = sel_use(u, slot, step)
                if step == "a3":
                    act.wait_ge(s_sel, filled)
                    if slot >= 0:
                        act.wait_ge(s_selE["D"], sel_use(u, slot, step)[2]["D"])
                    nc.scalar.activation(A3[0:PR, :], SEL[bank][0:PR, :], ACT.Copy).then_inc(s_selE["A"], 1)
                elif step == "xtok":
                    act.wait_ge(s_sel, filled)
                    if slot >= 0:
                        act.wait_ge(s_chain, STT * (TPG * (g - 1) + 1))
                        act.wait_ge(s_diag, TPG * (g - 1) + 1)
                    nc.scalar.activation(xtok[par][:, :, :], SEL[bank][:, 0:TPG * PR].rearrange(
                        "p (j r) -> p j r", r=PR)[:, :, 0:M], ACT.Copy).then_inc(s_selE["A"], 1)
                elif step[:2] == "xt":
                    q = int(step[2:])
                    act.wait_ge(s_sel, filled)
                    nc.scalar.activation(
                        XT[0:M, :].rearrange("p (b d) -> p d b", d=D)[:, 4 * q:4 * q + 4, :],
                        SEL[bank][0:M, :].rearrange("p (d b) -> p d b", b=P), ACT.Copy).then_inc(s_xthi, 1)
                elif step == "x1":
                    act.wait_ge(s_l0, NC0 * (g + 1))
                    nc.scalar.activation(x1hi[par][:, :], X1[:, :], ACT.Copy).then_inc(s_x1hi, 1)

            def copy_G(T):
                act.wait_ge(s_G, T + 3)
                nc.scalar.activation(
                    G[:, :, bass.ds((T + 1) * SB, SB)],
                    GB[:, 0:MH * SB].rearrange("p (m b) -> p m b", b=SB), ACT.Copy).then_inc(s_Gout, 1)

            act.wait_ge(s_const, 48)
            nc.scalar.activation(selw[:, :].rearrange("p (a n) -> p a n", a=2), selraw, ACT.Copy).then_inc(s_selw, 1)
            act.wait_ge(s_k1, 16)
            for c in range(NCH):
                nc.scalar.activation(k1hi[:, c * BANK:(c + 1) * BANK], k1raw[:, c, :], ACT.Copy).then_inc(s_k1hi, 1)
            nc.scalar.activation(credit[:, 2:3], ident[0:1, 0:1], ACT.Copy).then_inc(s_yA, NA)
            nc.scalar.activation(credit[:, 3:4], ident[0:1, 0:1], ACT.Copy).then_inc(s_Gout, 1)
            act.wait_ge(s_xtzero, 1)
            for step in prep_steps(True):
                prep(step, 0, -1)

            def body(u, last):
                for slot in range(GPB):
                    for p in range(TPG * NCH):
                        j, c = p // NCH, p % NCH
                        tile = slot * TPG + j
                        T = u * (GPB * TPG) + tile
                        if OWNER[c] == "A":
                            if rank(c) == 1:
                                act.wait_ge(s_sum, T + 1)
                                act.wait_ge(s_selE["A"], xtok_ready(u * GPB + slot))
                            act.wait_ge(s_y, NCH * T + c + 1)
                            for i in range(MB):
                                m = c * MB + i
                                ins = nc.scalar.activation(
                                    scaled[tile % 2][:, rank(c) - 1, i * O:(i + 1) * O],
                                    Y[(NCH * tile + c) % YB][:, i * O:(i + 1) * O], ACT.Copy,
                                    scale=xtok[slot % 2][:, j, m:m + 1])
                            ins.then_inc(s_yA, 1)
                        for step in steps_at(slot, last, p):
                            prep(step, u, slot)
                        if c == G_AT:
                            copy_G(T - 1)
            over_b_tiles(act, body)
            copy_G(NTILES - 1)
            act.wait_ge(s_z2, 1)
            nc.scalar.activation(z2, X1[:, :], ACT.Copy).then_inc(s_z2s, 1)
            act.wait_ge(s_mlp, 9 * 16)
            for i in range(H1 // P):
                act.wait_ge(s_h1, i + 1)
                nc.scalar.activation(h1[:, i, :], Y[i][:, :], ACT.Relu, bias=b1s[:, i:i + 1]).then_inc(s_h1s, 1)
            for i in range(H2 // P):
                act.wait_ge(s_h2, i + 1)
                nc.scalar.activation(h2[:, i, :], SEL[i][:, :], ACT.Relu, bias=b2s[:, i:i + 1]).then_inc(s_h2s, 1)
            act.wait_ge(s_yy, 1)
            nc.scalar.activation(ys[:, :], GB[0:1, :], ACT.Copy).then_inc(s_ys, 1)

        @block.vector
        def _(dve):
            def prep(step, u, slot):
                g, par = (u * GPB + slot + 1, (slot + 1) % 2) if slot >= 0 else (0, 0)
                if empties(step):
                    bank, filled, _, _ = sel_use(u, slot, step)
                if step[:4] == "roll":
                    c = int(step[4:])
                    dve.wait_ge(s_sel, filled)
                    dve.wait_ge(s_selE["A"], a3_ready(u, slot))
                    if slot >= 0 or c >= 2:
                        dve.wait_ge(s_l0, NC0 * g + c - 1)
                    nc.vector.tensor_tensor(prod[(g_odd(slot) + c) % 2][0:PR, :], SEL[bank][0:PR, :], A3[0:PR, :],
                                            ALU.mult).then_inc(s_selE["D"], 1)
                elif step[:2] == "xt" and step != "xtok":
                    q = int(step[2:])
                    dve.wait_ge(s_xthi, (4 * (u + 1) if slot >= 0 else 0) + q + 1)
                    nc.vector.tensor_tensor(
                        XT[LO:XR, :].rearrange("p (b d) -> p d b", d=D)[:, 4 * q:4 * q + 4, :],
                        SEL[bank][0:M, :].rearrange("p (d b) -> p d b", b=P),
                        XT[0:M, :].bitcast(f32).rearrange("p (b d) -> p d b", d=D)[:, 4 * q:4 * q + 4, :],
                        ALU.subtract).then_inc(s_selE["D"], 1)
                elif step == "x1":
                    dve.wait_ge(s_x1hi, g + 1)
                    nc.vector.tensor_tensor(x1lo[par][:, :], X1[:, :], x1hi[par][:, :].bitcast(f32),
                                            ALU.subtract).then_inc(s_x1lo, 1)
                    nc.vector.tensor_reduce(z0[:, bass.ds(g * (GROUP // D), GROUP // D)],
                                            X1[:, :].rearrange("p (b d) -> p b d", d=D), AX.X,
                                            ALU.add).then_inc(s_x1free, 1)

            def finish(T, buf):
                nc.vector.tensor_tensor(chain_sum[:, :], chain[buf][:, 0, :], chain[buf][:, 1, :],
                                        ALU.add).then_inc(s_csum, 1)
                dve.wait_ge(s_csum, T + 2)
                dve.wait_ge(s_sum, T + 3)
                nc.vector.tensor_tensor(x2[buf][:, :], chain_sum[:, :], scaled_sum[buf][:, :],
                                        ALU.add).then_inc(s_x2, 1)

            nc.vector.memset(XT[:, :].bitcast(f32), 0.0).then_inc(s_xtzero, 1)
            nc.vector.memset(x0g[:, M:MT, :], 0.0).then_inc(s_gzero, 1)
            nc.vector.memset(chain[1][:, :, :], 0.0).then_inc(s_chain, STT)
            nc.vector.memset(credit[:, 4:5], 0.0).then_inc(s_x2, 1)
            dve.wait_ge(s_w0, 32)
            nc.vector.tensor_tensor(w0[0:PR, 0:NC0 * O].rearrange("p (a n) -> p a n", a=2), w0a, w0b, ALU.add).then_inc(s_w0sum, 1)
            for c in range(NCH):
                dve.wait_ge(s_k1hi, c + 1)
                nc.vector.tensor_tensor(k1lo[:, c * BANK:(c + 1) * BANK], k1raw[:, c, :],
                                        k1hi[:, c * BANK:(c + 1) * BANK].bitcast(f32),
                                        ALU.subtract).then_inc(s_k1lo, 1)
            for step in prep_steps(True):
                prep(step, 0, -1)

            def body(u, last):
                for slot in range(GPB):
                    for p in range(TPG * NCH):
                        j, c = p // NCH, p % NCH
                        tile = slot * TPG + j
                        T = u * (GPB * TPG) + tile
                        if OWNER[c] == "D":
                            if rank(c) == 1:
                                dve.wait_ge(s_selE["A"], xtok_ready(u * GPB + slot))
                            dve.wait_ge(s_y, NCH * T + c + 1)
                            for i in range(MB):
                                m, n = c * MB + i, (rank(c) - 1) * MB + i
                                acc = chain[tile % 2][:, n % 2, :]
                                y = Y[(NCH * tile + c) % YB][:, i * O:(i + 1) * O]
                                e = xtok[slot % 2][:, j, m:m + 1]
                                if n < 2:
                                    nc.vector.tensor_scalar(acc, y, e, None, ALU.mult).then_inc(s_chain, 1)
                                else:
                                    dve.wait_ge(s_chain, STT * (T + 1) + n - 1)
                                    nc.vector.scalar_tensor_tensor(
                                        out=acc, in0=y, scalar=e, in1=acc, op0=ALU.mult,
                                        op1=ALU.add).then_inc(s_chain, 1)
                        for step in steps_at(slot, last, p):
                            prep(step, u, slot)
                        if c == FINISH_AT:
                            finish(T - 1, (tile - 1) % 2)
            over_b_tiles(dve, body)
            dve.wait_ge(s_chain, STT * (NTILES + 1))
            finish(NTILES - 1, (NTILES - 1) % 2)

        @block.tensor
        def _(pe):
            def prep(step, u, slot):
                g = u * GPB + slot + 1 if slot >= 0 else 0
                if empties(step):
                    bank, _, _, former = sel_use(u, slot, step)
                    if former:
                        pe.wait_ge(s_selE[former[0]], former[1])
                if step == "xtok":
                    pe.wait_ge(s_selE["A"], a3_ready(u, slot))
                    for j in range(TPG):
                        ins = nc.tensor.transpose(SEL[bank][:, j * PR:(j + 1) * PR], A3[0:PR, j * P:(j + 1) * P],
                                                  ident[0:PR, 0:PR])
                    ins.then_inc(s_sel, 1)
                elif step[:2] == "xt":
                    q, t = int(step[2:]), (u + 1 if slot >= 0 else 0)
                    if q == 0:
                        pe.wait_ge(s_gzero, 1)
                        pe.wait_ge(s_gather, 16 * M * (t + 1))
                    for i in range(4):
                        ins = nc.tensor.transpose(SEL[bank][0:MT, i * P:(i + 1) * P], x0g[:, :, 4 * q + i],
                                                  ident[:, :])
                    ins.then_inc(s_sel, 1)
                elif empties(step):
                    c = NC0 if step == "a3" else int(step[4:])
                    if step == "a3" and slot in (-1, GPB - 1):
                        pe.wait_ge(s_selE["D"], sel_use(u, slot, "xt3")[2]["D"])
                    cols = (slot + 1) % GPB * GROUP
                    nc.tensor.matmul(SEL[bank][0:PR, :], selw[:, c * PR:(c + 1) * PR], XT[:, cols:cols + GROUP],
                                     start=True, stop=True).then_inc(s_sel, 1)
                elif step[:3] == "l0_":
                    c = int(step[3:])
                    if c == 0 and slot >= 0:
                        pe.wait_ge(s_x1free, g)
                    pe.wait_ge(s_selE["D"], sel_use(u, slot, f"roll{c}")[2]["D"])
                    nc.tensor.matmul(X1[:, :], w0[0:PR, c * O:(c + 1) * O], prod[(g_odd(slot) + c) % 2][0:PR, :],
                                     start=(c == 0), stop=(c == NC0 - 1)).then_inc(s_l0, 1)

            def make_G(T, buf):
                pe.wait_ge(s_x2, T + 3)
                pe.wait_ge(s_diag, T + 2)
                pe.wait_ge(s_Gout, T + 2)
                nc.tensor.matmul(GB[:, 0:MH * SB], x2[buf][:, :], diag[buf][:, :, :].rearrange(
                    "p m b -> p (m b)"), start=True, stop=True).then_inc(s_G, 1)

            pe.wait_ge(s_const, 48)
            pe.wait_ge(s_selw, 1)
            pe.wait_ge(s_w0sum, 1)
            for step in prep_steps(True):
                prep(step, 0, -1)

            def body(u, last):
                for slot in range(GPB):
                    pe.wait_ge(s_x1lo, u * GPB + slot + 1)
                    if slot == 0:
                        pe.wait_ge(s_k1lo, NCH)
                    hi, lo = x1hi[slot % 2], x1lo[slot % 2]
                    for p in range(TPG * NCH):
                        j, c = p // NCH, p % NCH
                        tile = slot * TPG + j
                        T = u * (GPB * TPG) + tile
                        Tf, cf = (T, c - YB) if c >= YB else (T - 1, c - YB + NCH)
                        if OWNER[cf] == "A":
                            pe.wait_ge(s_yA, NA * (Tf + 1) + rank(cf))
                        else:
                            pe.wait_ge(s_chain, STT * (Tf + 1) + MB * rank(cf))
                        y = Y[(NCH * tile + c) % YB][:, :]
                        tok, cols = slice(j * P, (j + 1) * P), slice(c * BANK, (c + 1) * BANK)
                        nc.tensor.matmul(y, hi[:, tok], k1lo[:, cols], start=True, stop=False)
                        nc.tensor.matmul(y, hi[:, tok], k1hi[:, cols], start=False, stop=False)
                        nc.tensor.matmul(y, lo[:, tok], k1hi[:, cols], start=False, stop=True).then_inc(s_y, 1)
                        for step in steps_at(slot, last, p):
                            prep(step, u, slot)
                        if c == G_AT:
                            make_G(T - 1, (tile - 1) % 2)
            over_b_tiles(pe, body)
            make_G(NTILES - 1, (NTILES - 1) % 2)

            pe.wait_ge(s_mlp, 9 * 16)
            pe.wait_ge(s_chain, STT * (NTILES + 1))
            pe.wait_ge(s_yA, NA * (NTILES + 1))
            pe.wait_ge(s_x1free, BT * GPB)
            for i in range(H1 // P):
                o = slice(i * P, (i + 1) * P)
                nc.tensor.matmul(Y[i][:, :], w1s[0][:, o], z0[:, :], start=True, stop=False)
                nc.tensor.matmul(Y[i][:, :], w1cs[:, o], ctxs, start=False, stop=False)
            pe.wait_ge(s_k2, 16)
            pe.wait_ge(s_Gout, NTILES + 2)
            for i in range(H1 // P):
                nc.tensor.matmul(Y[i][:, :], w1s[1][:, i * P:(i + 1) * P], G[:, M, SB:], start=False, stop=False)
            for m in range(M):
                ins = nc.tensor.matmul(X1[:, :], k2s[:, m, :], G[:, m, SB:], start=(m == 0), stop=(m == M - 1))
            ins.then_inc(s_z2, 1)
            pe.wait_ge(s_z2s, 1)
            for i in range(H1 // P):
                nc.tensor.matmul(Y[i][:, :], w1s[2][:, i * P:(i + 1) * P], z2, start=False,
                                 stop=True).then_inc(s_h1, 1)
            for k in range(H1 // P):
                pe.wait_ge(s_h1s, k + 1)
                for i in range(H2 // P):
                    ins = nc.tensor.matmul(SEL[i][:, :], w2s[:, k, i * P:(i + 1) * P], h1[:, k, :],
                                           start=(k == 0), stop=(k == H1 // P - 1))
                    if k == H1 // P - 1:
                        ins.then_inc(s_h2, 1)
            for k in range(H2 // P):
                pe.wait_ge(s_h2s, k + 1)
                ins = nc.tensor.matmul(GB[0:1, :], w3s[:, k:k + 1], h2[:, k, :], start=(k == 0),
                                       stop=(k == H2 // P - 1))
            ins.then_inc(s_yy, 1)


def constants():
    import numpy as np
    sel = np.zeros((XR, NC0 + 1, PR), np.float32)
    for c in range(NC0 + 1):
        for kk in range(KC):
            for h in range(M):
                m = (h + (KC * c + kk if c < NC0 else 0)) % M
                sel[m, c, kk * M + h] = sel[LO + m, c, kk * M + h] = 1.0
    mask = (np.arange(P)[:, None] // D == np.arange(SB)[None, :]).astype(np.float32)
    return sel.reshape(XR, -1), np.eye(P, dtype=np.float32), mask


def kernel(**inputs):
    import numpy as np
    import concourse.bacc as bacc
    from concourse.bass_utils import run_bass_kernel_spmd

    a = {n: np.asarray(v) for n, v in inputs.items()}
    k0 = a["L0_rec_k0"].transpose(1, 2, 0)
    h = np.arange(M)
    k0a = np.zeros((KC, M, NC0, O), np.float32)
    k0b = np.zeros((KC, M, NC0, O), np.float32)
    for k in range(KD):
        k0a[k % KC, :, k // KC] = k0[h, (h + k) % M]
        if 0 < k < KD - 1:
            k0b[k % KC, :, k // KC] = k0[(h + k) % M, h]
    sel, ident, mask = constants()
    arrays = {
        "ids": a["ids"].reshape(BT, P, M).transpose(1, 0, 2),
        **{f"tbl_{m}": a[f"tbl_{m}"] for m in range(M)},
        "k0a": k0a.reshape(PR, NC0 * O), "k0b": k0b.reshape(PR, NC0 * O),
        "k1": a["L0_rec_k1"].transpose(1, 2, 0).reshape(O, M * O),
        "k2": a["L0_rec_k2"].transpose(1, 2, 0).reshape(O, M * O),
        "ctxT": a["dense_ctx"].T,
        "w1": a["W_top1"][:3 * P], "w1c": a["W_top1"][3 * P:], "b1": a["b_top1"].reshape(-1, P).T,
        "w2": a["W_top2"], "b2": a["b_top2"].reshape(-1, P).T, "w3": a["W_top3"].reshape(-1, P).T,
        "selw": sel, "ident": ident, "mask": mask,
    }
    arrays = {n: np.ascontiguousarray(v) for n, v in arrays.items()}
    nc = bacc.Bacc("TRN2", target_bir_lowering=False, num_devices=1)
    ap = {n: nc.dram_tensor("in_" + n, v.shape, mybir.dt.from_np(v.dtype), kind="ExternalInput").ap()
          for n, v in arrays.items()}
    out = nc.dram_tensor("out", (1, B), mybir.dt.float32, kind="ExternalOutput").ap()
    build(nc, ap["ids"], [ap[f"tbl_{m}"] for m in range(M)], ap["k0a"], ap["k0b"], ap["k1"], ap["k2"],
          ap["ctxT"], ap["w1"], ap["w1c"], ap["b1"], ap["w2"], ap["b2"], ap["w3"], ap["selw"],
          ap["ident"], ap["mask"], out)
    r = run_bass_kernel_spmd(nc, [{"in_" + n: v for n, v in arrays.items()}], core_ids=[0])
    return r.results[0]["out"].reshape(B, 1)
```

```python
import concourse.bass as bass
from concourse import mybir
from contextlib import ExitStack

B, M, D, O = 512, 40, 16, 128
P = 128
GROUP = 512
GS = GROUP // D
NG = B // GS
FQ = P // GS
GF = M // FQ
GPB = 4
BODIES = NG // GPB
TPG = GROUP // P
SB = P // D
NTILES = B * D // P
MH = M + 1
KD = M // 2 + 1
KC = 3
NC0 = KD // KC
PR = KC * M
ROLLS = M + KC * NC0 - 1
NR = 4
BANK = 512
MB = BANK // O
NCH = M // MB
YB = 5
OWNER = "ADADADADAD"
NA, ND = OWNER.count("A"), OWNER.count("D")
STT = ND * MB
FOLDS = NA - 2
MERGE = 3
CTX = 16
H1, H2 = 512, 256

XTOK_AT, PROD_AT, PROD_APART, L0_LAG = 14, 7, 4, 4
GATHER_TILES = 3
MERGE_AT = (3, 3, 3)
G_AT = 9


def position(step):
    if step == "xtok":
        return XTOK_AT
    if step == "x1":
        return position(f"l0_{NC0 - 1}") + 1
    kind, c = step[:-1], int(step[-1])
    return int(PROD_AT + PROD_APART * c) + (L0_LAG if kind == "l0_" else 0)


def prep_steps():
    names = ["xtok"] + [f"{kind}{c}" for kind in ("prod", "l0_") for c in range(NC0)] + ["x1"]
    return sorted(names, key=position)


def rank(c):
    return OWNER[:c + 1].count(OWNER[c])


def chunk(u, slot, c):
    k = NC0 * (slot + 1) + c
    return GPB * NC0 * u + k, k % NR, GPB * NC0 // NR * u + k // NR


def build(nc, ids, first_row, table, k0a, k0b, k1, k2, ctxT, w1, w1c, b1, w2, b2, w3, ident_in, mask_in, scratch, out):
    f32, f32r, i32 = mybir.dt.float32, mybir.dt.float32r, mybir.dt.int32
    ALU = mybir.AluOpType
    ACT = mybir.ActivationFunctionType
    AX = mybir.AxisListType
    ctx = ExitStack()
    where = {}
    with ctx:
        def sb(name, shape, dt=f32):
            t = ctx.enter_context(nc.sbuf_tensor(name, shape, dt))
            row = 4
            for n in shape[1:]:
                row *= n
            where[name] = nc.sbuf_base - -(-row // 32) * 32
            return t

        def over(home, name, shape, dt=f32, skip=0):
            return nc.alloc_sbuf_tensor_at(name, shape, dt, offset=where[home] + skip)

        def bank(name):
            return ctx.enter_context(nc.psum_tensor(name, [P, BANK], f32))

        def sem(name):
            return ctx.enter_context(nc.semaphore(name))

        idx = sb("idx", [P, NG, GF], i32)
        base = sb("base", [P, GF], i32)
        rows_now = [sb(f"rows_now{i}", [P, GF], i32) for i in range(2)]
        x0g = [sb(f"x0g{i}", [P, GF, D]) for i in range(2)]
        A3 = [sb(f"A3_{i}", [P, GROUP]) for i in range(2)]
        pairs = [sb(f"pairs{i}", [P, GROUP]) for i in range(NR)]
        x1hi = [sb(f"x1hi{i}", [P, GROUP], f32r) for i in range(2)]
        x1lo = [sb(f"x1lo{i}", [P, GROUP], f32r) for i in range(2)]
        xtok = [sb(f"xtok{i}", [P, TPG, M]) for i in range(2)]
        scaled = sb("scaled", [P, NA, BANK])
        fold = [sb(f"fold{i}", [P, BANK]) for i in range(2)]
        chain = [sb(f"chain{i}", [P, BANK]) for i in range(2)]
        x2 = [sb(f"x2_{i}", [P, O]) for i in range(2)]
        diag = [sb(f"diag{i}", [P, MH, SB]) for i in range(2)]
        G = sb("G", [P, MH, SB + B])
        z0 = sb("z0", [P, B])
        k1hi = sb("k1hi", [P, M * O], f32r)
        k1lo = sb("k1lo", [P, M * O], f32r)
        k2s = sb("k2s", [P, M, O])
        w0 = sb("w0", [PR, NC0 * O])
        ident = sb("ident", [P, P])
        mask = sb("mask", [P, SB])
        credit = sb("credit", [1, 8])
        w3s = sb("w3s", [P, H2 // P])
        b1s = sb("b1s", [P, H1 // P])
        b2s = sb("b2s", [P, H2 // P])
        k1raw = over("G", "k1raw", [P, NCH, BANK])
        w0a, w0b = (over("G", f"w0{n}", [PR, NC0 * O], skip=4 * (NCH * BANK + i * NC0 * O))
                    for i, n in enumerate(("a", "b")))
        w1s = pairs
        w1cs, ctxs = A3[0][0:CTX, :], A3[1][0:CTX, :]
        z2, w2s = pairs[3], sb("w2s", [P, H1 // P, H2])
        h1 = scaled
        h2, ys = G[:, 0:2, 0:B], G[0:1, 2, 0:B]

        Y = [bank(f"Y{i}") for i in range(YB)]
        SEL = bank("SEL")
        X1 = bank("X1")
        GB = bank("GB")
        H = [SEL, Y[YB - 1]]

        s_idx, s_k1, s_const, s_w0, s_mlp, s_k2 = [sem(n) for n in (
            "idx_in", "k1_in", "const_in", "w0_in", "mlp_in", "k2_in")]
        s_gather, s_rows = [sem(f"gathered{i}") for i in range(2)], sem("rows_ready")
        s_k1hi, s_k1lo, s_w0sum, s_dzero, s_dones = [sem(n) for n in (
            "k1hi_ready", "k1lo_ready", "w0_summed", "diag_zeroed", "diag_ones")]
        s_sel = sem("sel_filled")
        s_selE = sem("sel_emptied")
        s_scratch, s_again, s_a3 = sem("scratch_written"), sem("scratch_repeated"), sem("a3_in")
        s_roll = [sem(f"rolled_in{i}") for i in range(NR)]
        s_prod, s_l0 = sem("products_ready"), sem("l0_done")
        s_x1hi, s_x1lo, s_x1free = sem("x1_high_ready"), sem("x1_low_ready"), sem("x1_bank_free")
        s_y, s_yA = sem("y_filled"), sem("y_emptied_by_act")
        s_chain = sem("chain_steps")
        s_fold = sem("pool_folds")
        s_merge = sem("tile_sums_merged")
        s_diag, s_G, s_Gout = sem("diag_ready"), sem("g_filled"), sem("g_copied")
        s_z2, s_z2s, s_h1, s_h1s, s_h2, s_h2s, s_yy, s_ys, s_out = [sem(n) for n in (
            "z2_filled", "z2_ready", "h1_filled", "h1_ready", "h2_filled", "h2_ready", "out_filled",
            "out_ready", "stored")]

        block = ctx.enter_context(nc.Block())

        def over_groups(eng, body):
            with eng.Fori(0, BODIES - 1) as u:
                body(u, False)
            body(BODIES - 1, True)

        def steps_at(slot, last, p):
            return [] if last and slot == GPB - 1 else [n for n in prep_steps() if position(n) == p]

        @block.sync
        def _(sp):
            sp.dma_start(idx[:, :, :], ids).then_inc(s_idx, 16)
            sp.dma_start(base[:, :], first_row).then_inc(s_idx, 16)
            sp.dma_start(ident[:, :], ident_in).then_inc(s_const, 16)
            sp.dma_start(mask[:, :], mask_in).then_inc(s_const, 16)
            sp.dma_start(k1raw[:, :, :], k1.rearrange("h (c n) -> h c n", n=BANK)).then_inc(s_k1, 16)
            sp.dma_start(w0a[:, :], k0a).then_inc(s_w0, 16)
            sp.dma_start(w0b[:, :], k0b).then_inc(s_w0, 16)
            sp.dma_start(w3s[:, :], w3).then_inc(s_mlp, 16)
            sp.dma_start(b1s[:, :], b1).then_inc(s_mlp, 16)
            sp.dma_start(b2s[:, :], b2).then_inc(s_mlp, 16)

            def spread(u, slot):
                g, par = u * GPB + slot + 1, (slot + 1) % 2

                def rows(first, step):
                    return bass.AP(scratch.tensor, (par * ROLLS + first) * GROUP,
                                   [[step * GROUP, KC], [GROUP, M], [1, GROUP]])
                sp.wait_ge(s_gather[par], 16 * GF * (GPB // 2 * u + (slot + 1) // 2 + 1))
                for q in range(FQ):
                    sp.dma_start(scratch[par, q * GF:(q + 1) * GF, :].rearrange("f (b d) -> b f d", d=D),
                                 x0g[par][q * GS:(q + 1) * GS, :, :]).then_inc(s_scratch, 16)
                sp.wait_ge(s_scratch, 16 * FQ * (g + 1))
                sp.dma_start(scratch[par, M:ROLLS, :], scratch[par, 0:ROLLS - M, :]).then_inc(s_again, 16)
                sp.wait_ge(s_again, 16 * (g + 1))
                sp.dma_start(A3[par][0:PR, :], rows(0, 0)).then_inc(s_a3, 16)
                for c in range(NC0):
                    n, buf, _ = chunk(u, slot, c)
                    if slot >= 0 or c >= NR:
                        sp.wait_ge(s_l0, n - NR + 1)
                    sp.dma_start(pairs[buf][0:PR, :], rows(KC * c, 1)).then_inc(s_roll[buf], 16)

            spread(0, -1)
            sp.dma_start(k2s[:, :, :], k2.rearrange("h (m o) -> h m o", o=O)).then_inc(s_k2, 16)

            def body(u, last):
                for slot in range(GPB - last):
                    spread(u, slot)
            over_groups(sp, body)

            sp.wait_ge(s_x1free, NG)
            for k in range(3):
                sp.dma_start(w1s[k][:, :], w1[k * P:(k + 1) * P, :]).then_inc(s_mlp, 16)
            sp.dma_start(w1cs[:, :], w1c).then_inc(s_mlp, 16)
            sp.dma_start(ctxs[:, :], ctxT).then_inc(s_mlp, 16)
            sp.dma_start(w2s[:, :, :], w2.rearrange("(c p) n -> p c n", p=P)).then_inc(s_mlp, 16)
            sp.wait_ge(s_ys, 1)
            sp.dma_start(out, ys).then_inc(s_out, 16)
            sp.wait_ge(s_out, 16)

        @block.gpsimd
        def _(pool):
            def take_rows(g, buf):
                nc.gpsimd.tensor_tensor(rows_now[buf][:, :], idx[:, g, :], base[:, :], ALU.add).then_inc(s_rows, 1)
                pool.wait_ge(s_rows, g + 1)

            def gather(buf, fields):
                for f in fields:
                    nc.gpsimd.indirect_dma_start(
                        x0g[buf][:, f, :], None, table,
                        bass.IndirectOffsetOnAxis(ap=rows_now[buf][:, f:f + 1], axis=0)).then_inc(s_gather[buf], 16)

            pool.wait_ge(s_idx, 32)
            for g in range(2):
                take_rows(g, g)
                gather(g, range(GF))
            for i in range(2):
                nc.gpsimd.memset(diag[i][:, :, :], 0.0).then_inc(s_dzero, 1)
            pool.wait_ge(s_dzero, 2)
            pool.wait_ge(s_const, 32)
            for i in range(2):
                nc.gpsimd.tensor_copy(diag[i][:, M, :], mask[:, :]).then_inc(s_dones, 1)
            pool.wait_ge(s_dones, 2)
            nc.gpsimd.memset(fold[1][:, :], 0.0).then_inc(s_fold, FOLDS)
            nc.gpsimd.memset(credit[:, 0:1], 0.0).then_inc(s_G, 1)
            nc.gpsimd.memset(credit[:, 1:2], 0.0).then_inc(s_diag, 1)
            def body(u, last):
                for tile in range(GPB * TPG):
                    slot, j = tile // TPG, tile % TPG
                    T = u * (GPB * TPG) + tile
                    gathers = not last or slot < GPB - 2
                    if gathers and j == 0:
                        pool.wait_ge(s_prod, NC0 * (u * GPB + slot + 1))
                        take_rows(u * GPB + slot + 2, slot % 2)
                    pool.wait_ge(s_selE, u * GPB + slot + 1)
                    pool.wait_ge(s_G, T + 1)
                    nc.gpsimd.tensor_tensor(
                        diag[tile % 2][:, 0:M, :],
                        xtok[slot % 2][:, j, :].unsqueeze(2).to_broadcast([P, M, SB]),
                        mask[:, :].unsqueeze(1).to_broadcast([P, M, SB]), ALU.mult).then_inc(s_diag, 1)
                    sums = fold[tile % 2]
                    pool.wait_ge(s_merge, MERGE * T + 1)
                    for a in range(2, NA):
                        pool.wait_ge(s_yA, NA * (T + 1) + a + 1)
                        if a > 2:
                            pool.wait_ge(s_fold, FOLDS * (T + 1) + a - 2)
                        nc.gpsimd.tensor_tensor(sums[:, :], scaled[:, 1, :] if a == 2 else sums[:, :],
                                                scaled[:, a, :], ALU.add).then_inc(s_fold, 1)
                    if gathers and j < GATHER_TILES:
                        gather(slot % 2, range(-(-GF * j // GATHER_TILES), -(-GF * (j + 1) // GATHER_TILES)))
            over_groups(pool, body)

        @block.scalar
        def _(act):
            def prep(step, u, slot):
                g, par = (u * GPB + slot + 1, (slot + 1) % 2) if slot >= 0 else (0, 0)
                if step == "xtok":
                    act.wait_ge(s_sel, g + 1)
                    if slot >= 0:
                        act.wait_ge(s_chain, STT * (TPG * (g - 1) + 1))
                        act.wait_ge(s_diag, TPG * (g - 1) + 1)
                    nc.scalar.activation(xtok[par][:, :, :], SEL[:, 0:TPG * PR].rearrange(
                        "p (j r) -> p j r", r=PR)[:, :, 0:M], ACT.Copy).then_inc(s_selE, 1)
                elif step == "x1":
                    act.wait_ge(s_l0, NC0 * (g + 1))
                    nc.scalar.activation(x1hi[par][:, :], X1[:, :], ACT.Copy).then_inc(s_x1hi, 1)

            def copy_G(T):
                act.wait_ge(s_G, T + 3)
                nc.scalar.activation(
                    G[:, :, bass.ds((T + 1) * SB, SB)],
                    GB[:, 0:MH * SB].rearrange("p (m b) -> p m b", b=SB), ACT.Copy).then_inc(s_Gout, 1)

            act.wait_ge(s_const, 32)
            act.wait_ge(s_k1, 16)
            for c in range(NCH):
                nc.scalar.activation(k1hi[:, c * BANK:(c + 1) * BANK], k1raw[:, c, :], ACT.Copy).then_inc(s_k1hi, 1)
            nc.scalar.activation(credit[:, 2:3], ident[0:1, 0:1], ACT.Copy).then_inc(s_yA, NA)
            nc.scalar.activation(credit[:, 3:4], ident[0:1, 0:1], ACT.Copy).then_inc(s_Gout, 1)
            for step in prep_steps():
                prep(step, 0, -1)

            def body(u, last):
                for slot in range(GPB):
                    for p in range(TPG * NCH):
                        j, c = p // NCH, p % NCH
                        tile = slot * TPG + j
                        T = u * (GPB * TPG) + tile
                        if OWNER[c] == "A":
                            if rank(c) == 1:
                                act.wait_ge(s_chain, STT * T + MB)
                            else:
                                act.wait_ge(s_fold, FOLDS * T + max(rank(c) - 2, 1))
                            if rank(c) == 1:
                                act.wait_ge(s_selE, u * GPB + slot + 1)
                            act.wait_ge(s_y, NCH * T + c + 1)
                            for i in range(MB):
                                m = c * MB + i
                                ins = nc.scalar.activation(
                                    scaled[:, rank(c) - 1, i * O:(i + 1) * O],
                                    Y[(NCH * tile + c) % YB][:, i * O:(i + 1) * O], ACT.Copy,
                                    scale=xtok[slot % 2][:, j, m:m + 1])
                            ins.then_inc(s_yA, 1)
                        for step in steps_at(slot, last, p):
                            prep(step, u, slot)
                        if c == G_AT:
                            copy_G(T - 1)
            over_groups(act, body)
            copy_G(NTILES - 1)
            act.wait_ge(s_z2, 1)
            nc.scalar.activation(z2[:, :], X1[:, :], ACT.Copy).then_inc(s_z2s, 1)
            act.wait_ge(s_mlp, 9 * 16)
            for i in range(H1 // P):
                act.wait_ge(s_h1, i + 1)
                nc.scalar.activation(h1[:, i, :], Y[i][:, :], ACT.Relu, bias=b1s[:, i:i + 1]).then_inc(s_h1s, 1)
            for i in range(H2 // P):
                act.wait_ge(s_h2, i + 1)
                nc.scalar.activation(h2[:, i, :], H[i][:, :], ACT.Relu, bias=b2s[:, i:i + 1]).then_inc(s_h2s, 1)
            act.wait_ge(s_yy, 1)
            nc.scalar.activation(ys, GB[0:1, :], ACT.Copy).then_inc(s_ys, 1)

        @block.vector
        def _(dve):
            def prep(step, u, slot):
                g, par = (u * GPB + slot + 1, (slot + 1) % 2) if slot >= 0 else (0, 0)
                if step[:4] == "prod":
                    _, buf, fills = chunk(u, slot, int(step[4:]))
                    dve.wait_ge(s_a3, 16 * (g + 1))
                    dve.wait_ge(s_roll[buf], 16 * (fills + 1))
                    nc.vector.tensor_tensor(pairs[buf][0:PR, :], pairs[buf][0:PR, :], A3[par][0:PR, :],
                                            ALU.mult).then_inc(s_prod, 1)
                elif step == "x1":
                    dve.wait_ge(s_x1hi, g + 1)
                    nc.vector.tensor_tensor(x1lo[par][:, :], X1[:, :], x1hi[par][:, :].bitcast(f32),
                                            ALU.subtract).then_inc(s_x1lo, 1)
                    nc.vector.tensor_reduce(z0[:, bass.ds(g * (GROUP // D), GROUP // D)],
                                            X1[:, :].rearrange("p (b d) -> p b d", d=D), AX.X,
                                            ALU.add).then_inc(s_x1free, 1)

            def merge(T, par, k):
                sums = chain[par]
                if k == 0:
                    dve.wait_ge(s_chain, STT * (T + 2))
                    dve.wait_ge(s_fold, FOLDS * (T + 2))
                    a, b, to = sums[:, :], fold[par][:, :], sums[:, :]
                else:
                    dve.wait_ge(s_merge, MERGE * (T + 2) + k)
                    n = BANK >> k
                    a, b = sums[:, 0:n], sums[:, n:2 * n]
                    to = sums[:, 0:n] if k < MERGE - 1 else x2[par][:, :]
                nc.vector.tensor_tensor(to, a, b, ALU.add).then_inc(s_merge, 1)

            nc.vector.memset(chain[1][:, :], 0.0).then_inc(s_chain, STT)
            nc.vector.memset(credit[:, 4:5], 0.0).then_inc(s_merge, MERGE)
            dve.wait_ge(s_w0, 32)
            nc.vector.tensor_tensor(w0[:, :], w0a[:, :], w0b[:, :], ALU.add).then_inc(s_w0sum, 1)
            for c in range(NCH):
                dve.wait_ge(s_k1hi, c + 1)
                nc.vector.tensor_tensor(k1lo[:, c * BANK:(c + 1) * BANK], k1raw[:, c, :],
                                        k1hi[:, c * BANK:(c + 1) * BANK].bitcast(f32),
                                        ALU.subtract).then_inc(s_k1lo, 1)
            for step in prep_steps():
                prep(step, 0, -1)

            def body(u, last):
                for slot in range(GPB):
                    for p in range(TPG * NCH):
                        j, c = p // NCH, p % NCH
                        tile = slot * TPG + j
                        T = u * (GPB * TPG) + tile
                        if OWNER[c] == "D":
                            if rank(c) == 1:
                                dve.wait_ge(s_selE, u * GPB + slot + 1)
                                dve.wait_ge(s_merge, MERGE * (T + 1))
                                dve.wait_ge(s_yA, NA * (T + 1) + 1)
                            dve.wait_ge(s_y, NCH * T + c + 1)
                            for i in range(MB):
                                m, n = c * MB + i, (rank(c) - 1) * MB + i
                                if n >= MB:
                                    dve.wait_ge(s_chain, STT * (T + 1) + n - MB + 1)
                                nc.vector.scalar_tensor_tensor(
                                    out=chain[tile % 2][:, i * O:(i + 1) * O], in0=Y[(NCH * tile + c) % YB][:, i * O:(i + 1) * O],
                                    scalar=xtok[slot % 2][:, j, m:m + 1],
                                    in1=chain[tile % 2][:, i * O:(i + 1) * O] if n >= MB else scaled[:, 0, i * O:(i + 1) * O],
                                    op0=ALU.mult, op1=ALU.add).then_inc(s_chain, 1)
                        for step in steps_at(slot, last, p):
                            prep(step, u, slot)
                        for k in range(MERGE):
                            if c == MERGE_AT[k]:
                                merge(T - 1, (tile - 1) % 2, k)
            over_groups(dve, body)
            for k in range(MERGE):
                merge(NTILES - 1, (NTILES - 1) % 2, k)

        @block.tensor
        def _(pe):
            def prep(step, u, slot):
                g = u * GPB + slot + 1 if slot >= 0 else 0
                if step == "xtok":
                    pe.wait_ge(s_a3, 16 * (g + 1))
                    if slot >= 0:
                        pe.wait_ge(s_selE, g)
                    for j in range(TPG):
                        ins = nc.tensor.transpose(SEL[:, j * PR:(j + 1) * PR],
                                                  A3[(slot + 1) % 2][0:PR, j * P:(j + 1) * P], ident[0:PR, 0:PR])
                    ins.then_inc(s_sel, 1)
                elif step[:3] == "l0_":
                    c = int(step[3:])
                    n, buf, _ = chunk(u, slot, c)
                    if c == 0 and slot >= 0:
                        pe.wait_ge(s_x1free, g)
                    pe.wait_ge(s_prod, n + 1)
                    nc.tensor.matmul(X1[:, :], w0[:, c * O:(c + 1) * O], pairs[buf][0:PR, :],
                                     start=(c == 0), stop=(c == NC0 - 1)).then_inc(s_l0, 1)

            def make_G(T, buf):
                pe.wait_ge(s_merge, MERGE * (T + 3))
                pe.wait_ge(s_diag, T + 2)
                pe.wait_ge(s_Gout, T + 2)
                nc.tensor.matmul(GB[:, 0:MH * SB], x2[buf][:, :], diag[buf][:, :, :].rearrange(
                    "p m b -> p (m b)"), start=True, stop=True).then_inc(s_G, 1)

            pe.wait_ge(s_const, 32)
            pe.wait_ge(s_w0sum, 1)
            for step in prep_steps():
                prep(step, 0, -1)

            def body(u, last):
                for slot in range(GPB):
                    pe.wait_ge(s_x1lo, u * GPB + slot + 1)
                    if slot == 0:
                        pe.wait_ge(s_k1lo, NCH)
                    hi, lo = x1hi[slot % 2], x1lo[slot % 2]
                    for p in range(TPG * NCH):
                        j, c = p // NCH, p % NCH
                        tile = slot * TPG + j
                        T = u * (GPB * TPG) + tile
                        Tf, cf = (T, c - YB) if c >= YB else (T - 1, c - YB + NCH)
                        if OWNER[cf] == "A":
                            pe.wait_ge(s_yA, NA * (Tf + 1) + rank(cf))
                        else:
                            pe.wait_ge(s_chain, STT * (Tf + 1) + MB * rank(cf))
                        y = Y[(NCH * tile + c) % YB][:, :]
                        tok, cols = slice(j * P, (j + 1) * P), slice(c * BANK, (c + 1) * BANK)
                        nc.tensor.matmul(y, hi[:, tok], k1lo[:, cols], start=True, stop=False)
                        nc.tensor.matmul(y, hi[:, tok], k1hi[:, cols], start=False, stop=False)
                        nc.tensor.matmul(y, lo[:, tok], k1hi[:, cols], start=False, stop=True).then_inc(s_y, 1)
                        for step in steps_at(slot, last, p):
                            prep(step, u, slot)
                        if c == G_AT:
                            make_G(T - 1, (tile - 1) % 2)
            over_groups(pe, body)
            make_G(NTILES - 1, (NTILES - 1) % 2)

            pe.wait_ge(s_mlp, 9 * 16)
            pe.wait_ge(s_chain, STT * (NTILES + 1))
            pe.wait_ge(s_yA, NA * (NTILES + 1))
            pe.wait_ge(s_x1free, NG)
            for i in range(H1 // P):
                o = slice(i * P, (i + 1) * P)
                nc.tensor.matmul(Y[i][:, :], w1s[0][:, o], z0[:, :], start=True, stop=False)
                nc.tensor.matmul(Y[i][:, :], w1cs[:, o], ctxs[:, :], start=False, stop=False)
            pe.wait_ge(s_k2, 16)
            pe.wait_ge(s_Gout, NTILES + 2)
            for i in range(H1 // P):
                nc.tensor.matmul(Y[i][:, :], w1s[1][:, i * P:(i + 1) * P], G[:, M, SB:], start=False, stop=False)
            for m in range(M):
                ins = nc.tensor.matmul(X1[:, :], k2s[:, m, :], G[:, m, SB:], start=(m == 0), stop=(m == M - 1))
            ins.then_inc(s_z2, 1)
            pe.wait_ge(s_z2s, 1)
            for i in range(H1 // P):
                nc.tensor.matmul(Y[i][:, :], w1s[2][:, i * P:(i + 1) * P], z2[:, :], start=False,
                                 stop=True).then_inc(s_h1, 1)
            for k in range(H1 // P):
                pe.wait_ge(s_h1s, k + 1)
                for i in range(H2 // P):
                    ins = nc.tensor.matmul(H[i][:, :], w2s[:, k, i * P:(i + 1) * P], h1[:, k, :],
                                           start=(k == 0), stop=(k == H1 // P - 1))
                    if k == H1 // P - 1:
                        ins.then_inc(s_h2, 1)
            for k in range(H2 // P):
                pe.wait_ge(s_h2s, k + 1)
                ins = nc.tensor.matmul(GB[0:1, :], w3s[:, k:k + 1], h2[:, k, :], start=(k == 0),
                                       stop=(k == H2 // P - 1))
            ins.then_inc(s_yy, 1)


def first_rows(lengths):
    import numpy as np
    first = np.cumsum([0] + lengths[:-1]).astype(np.int32)
    return np.repeat(first.reshape(FQ, 1, GF), GS, axis=1).reshape(P, GF)


def constants():
    import numpy as np
    mask = (np.arange(P)[:, None] // D == np.arange(SB)[None, :]).astype(np.float32)
    return np.eye(P, dtype=np.float32), mask


def kernel(**inputs):
    import numpy as np
    import concourse.bacc as bacc
    from concourse.bass_utils import run_bass_kernel_spmd

    a = {n: np.asarray(v) for n, v in inputs.items()}
    k0 = a["L0_rec_k0"].transpose(1, 2, 0)
    h = np.arange(M)
    k0a = np.zeros((KC, M, NC0, O), np.float32)
    k0b = np.zeros((KC, M, NC0, O), np.float32)
    for k in range(KD):
        k0a[k % KC, :, k // KC] = k0[h, (h + k) % M]
        if 0 < k < KD - 1:
            k0b[k % KC, :, k // KC] = k0[(h + k) % M, h]
    ident, mask = constants()
    arrays = {
        "ids": a["ids"].reshape(NG, GS, FQ, GF).transpose(2, 1, 0, 3).reshape(P, NG, GF),
        "table": np.concatenate([a[f"tbl_{m}"] for m in range(M)]),
        "first_row": first_rows([len(a[f"tbl_{m}"]) for m in range(M)]),
        "k0a": k0a.reshape(PR, NC0 * O), "k0b": k0b.reshape(PR, NC0 * O),
        "k1": a["L0_rec_k1"].transpose(1, 2, 0).reshape(O, M * O),
        "k2": a["L0_rec_k2"].transpose(1, 2, 0).reshape(O, M * O),
        "ctxT": a["dense_ctx"].T,
        "w1": a["W_top1"][:3 * P], "w1c": a["W_top1"][3 * P:], "b1": a["b_top1"].reshape(-1, P).T,
        "w2": a["W_top2"], "b2": a["b_top2"].reshape(-1, P).T, "w3": a["W_top3"].reshape(-1, P).T,
        "ident": ident, "mask": mask,
    }
    arrays = {n: np.ascontiguousarray(v) for n, v in arrays.items()}
    nc = bacc.Bacc("TRN2", target_bir_lowering=False, num_devices=1)
    ap = {n: nc.dram_tensor("in_" + n, v.shape, mybir.dt.from_np(v.dtype), kind="ExternalInput").ap()
          for n, v in arrays.items()}
    out = nc.dram_tensor("out", (1, B), mybir.dt.float32, kind="ExternalOutput").ap()
    scratch = nc.dram_tensor("scratch", (2, ROLLS, GROUP), mybir.dt.float32, kind="Internal").ap()
    build(nc, ap["ids"], ap["first_row"], ap["table"], ap["k0a"], ap["k0b"], ap["k1"], ap["k2"],
          ap["ctxT"], ap["w1"], ap["w1c"], ap["b1"], ap["w2"], ap["b2"], ap["w3"], ap["ident"],
          ap["mask"], scratch, out)
    r = run_bass_kernel_spmd(nc, [{"in_" + n: v for n, v in arrays.items()}], core_ids=[0])
    return r.results[0]["out"].reshape(B, 1)
```

```python
import concourse.bass as bass
from concourse import mybir
from contextlib import ExitStack

B, M, D, O = 512, 40, 16, 128
P = 128
GROUP = 512
GS = GROUP // D
NG = B // GS
FQ = P // GS
GF = M // FQ
GPB = 4
BODIES = NG // GPB
TPG = GROUP // P
SB = P // D
NTILES = B * D // P
MH = M + 1
KD = M // 2 + 1
KC = 3
NC0 = KD // KC
PR = KC * M
ROLLS = M + KC * NC0 - 1
NH = 3
NR = 4
BANK = 512
MB = BANK // O
NCH = M // MB
YB = 5
OWNER = "ADAADAADAD"
NA, ND = OWNER.count("A"), OWNER.count("D")
STT = ND * MB
FOLDS = 3
EXTRA = NA - 2 - FOLDS
MERGE = EXTRA + 3
NS = 3
CTX = 16
H1, H2 = 512, 256

XTOK_AT, PROD_AT, PROD_APART, L0_LAG = 14, 6, 3.6, 6
SPLIT_LAG = {"ph": 1, "pl": 2}
X1_LAG = {"x1hi": 1, "x1lo": 2, "z0": 3}
GATHER_TILES = 3
MERGE_AT = (0, 3, 3, 3)
G_AT = 8


def position(step):
    if step == "xtok":
        return XTOK_AT
    if step in X1_LAG:
        return position(f"l0_{NC0 - 1}") + X1_LAG[step]
    kind, c = step[:-1], int(step[-1])
    if kind in ("l0_", "prod"):
        return int(PROD_AT + PROD_APART * c) + (L0_LAG if kind == "l0_" else 0)
    return int(PROD_AT + PROD_APART * c) + SPLIT_LAG[kind]


def prep_steps():
    names = ["xtok"]
    for kind, n in (("prod", NC0), ("ph", NS), ("pl", NS), ("l0_", NC0)):
        names += [f"{kind}{c}" for c in range(n)]
    names += X1_LAG
    return sorted(names, key=position)


def rank(c):
    return OWNER[:c + 1].count(OWNER[c])


def chunk(u, slot, c):
    k = NC0 * (slot + 1) + c
    return GPB * NC0 * u + k, k % NR, GPB * NC0 // NR * u + k // NR


def split(u, slot, c):
    k = NS * (slot + 1) + c
    number = NC0 * (GPB * u + slot + 1) + c
    free = number - NH + 1 if c >= NH else number - NC0 + NS - NH + 1 if slot >= 0 else None
    return GPB * NS * u + k, k % NH, free


def build(nc, ids, first_row, table, k0a, k0b, k1, k2, ctxT, w1, w1c, b1, w2, b2, w3, ident_in, mask_in,
          scratch, out):
    f32, f32r, i32 = mybir.dt.float32, mybir.dt.float32r, mybir.dt.int32
    ALU = mybir.AluOpType
    ACT = mybir.ActivationFunctionType
    AX = mybir.AxisListType
    ctx = ExitStack()
    where = {}
    with ctx:
        def sb(name, shape, dt=f32):
            t = ctx.enter_context(nc.sbuf_tensor(name, shape, dt))
            row = 4
            for n in shape[1:]:
                row *= n
            where[name] = nc.sbuf_base - -(-row // 32) * 32
            return t

        def over(home, name, shape, dt=f32, skip=0):
            return nc.alloc_sbuf_tensor_at(name, shape, dt, offset=where[home] + skip)

        def bank(name):
            return ctx.enter_context(nc.psum_tensor(name, [P, BANK], f32))

        def sem(name):
            return ctx.enter_context(nc.semaphore(name))

        idx = sb("idx", [P, NG, GF], i32)
        base = sb("base", [P, GF], i32)
        rows_now = [sb(f"rows_now{i}", [P, GF], i32) for i in range(2)]
        x0g = [sb(f"x0g{i}", [P, GF, D]) for i in range(2)]
        A3 = [sb(f"A3_{i}", [P, GROUP]) for i in range(2)]
        pairs = [sb(f"pairs{i}", [P, GROUP]) for i in range(NR)]
        pairs_lo = [over(f"pairs{i}", f"pairs_lo{i}", [P, GROUP], f32r) for i in range(NR)]
        pairs_hi = [sb(f"pairs_hi{i}", [P, GROUP], f32r) for i in range(NH)]
        x1hi = [sb(f"x1hi{i}", [P, GROUP], f32r) for i in range(2)]
        x1lo = [sb(f"x1lo{i}", [P, GROUP], f32r) for i in range(2)]
        xtok = [sb(f"xtok{i}", [P, TPG, M]) for i in range(2)]
        scaled = sb("scaled", [P, NA, BANK])
        fold = [sb(f"fold{i}", [P, BANK]) for i in range(2)]
        chain = [sb(f"chain{i}", [P, BANK]) for i in range(2)]
        x2 = [sb(f"x2_{i}", [P, O]) for i in range(2)]
        diag = [sb(f"diag{i}", [P, MH, SB]) for i in range(2)]
        G = sb("G", [P, MH, SB + B])
        z0 = sb("z0", [P, B])
        k1hi = sb("k1hi", [P, M * O], f32r)
        k1lo = sb("k1lo", [P, M * O], f32r)
        k2s = sb("k2s", [P, M, O])
        w0hi = sb("w0hi", [PR, NS * O], f32r)
        w0lo = sb("w0lo", [PR, NS * O], f32r)
        w0 = sb("w0", [PR, max(NC0 - NS, 1) * O])
        ident = sb("ident", [P, P])
        mask = sb("mask", [P, SB])
        credit = sb("credit", [1, 8])
        w3s = sb("w3s", [P, H2 // P])
        b1s = sb("b1s", [P, H1 // P])
        b2s = sb("b2s", [P, H2 // P])
        k1raw = over("G", "k1raw", [P, NCH, BANK])
        w0a, w0b, w0s = (over("G", f"w0{n}", [PR, NC0 * O], skip=4 * (NCH * BANK + i * NC0 * O))
                         for i, n in enumerate(("a", "b", "s")))
        w1s = pairs
        w1cs, ctxs = A3[0][0:CTX, :], A3[1][0:CTX, :]
        z2, w2s = pairs[3], over("fold0", "w2s", [P, H1 // P, H2])
        h1 = scaled[:, 0:H1 // P, :]
        k2hi, k2lo = k1hi, k1lo
        Ghi = x1hi + pairs_hi[0:2]
        Glo = x1lo + [pairs_hi[2], over("chain0", "Glo3", [P, B], f32r)]
        h2, ys = G[:, 0:2, 0:B], G[0:1, 2, 0:B]

        Y = [bank(f"Y{i}") for i in range(YB)]
        TR = bank("TR")
        X1 = bank("X1")
        GB = bank("GB")
        H = [TR, Y[YB - 1]]

        s_idx, s_k1, s_const, s_w0, s_mlp, s_w2, s_k2 = [sem(n) for n in (
            "idx_in", "k1_in", "const_in", "w0_in", "mlp_in", "w2_in", "k2_in")]
        s_gather, s_rows = [sem(f"gathered{i}") for i in range(2)], sem("rows_ready")
        s_k1hi, s_k1lo, s_w0sum, s_dzero, s_dones, s_szero = [sem(n) for n in (
            "k1hi_ready", "k1lo_ready", "w0_summed", "diag_zeroed", "diag_ones", "scaled_zeroed")]
        s_trans = sem("tokens_transposed")
        s_xtok = sem("xtok_ready")
        s_scratch, s_again, s_a3 = sem("scratch_written"), sem("scratch_repeated"), sem("a3_in")
        s_roll = [sem(f"rolled_in{i}") for i in range(NR)]
        s_prod, s_ph, s_pl, s_l0 = [sem(n) for n in (
            "products_ready", "high_products_ready", "low_products_ready", "l0_done")]
        s_w0hi, s_w0lo = sem("w0hi_ready"), sem("w0lo_ready")
        s_x1hi, s_x1lo, s_x1free = sem("x1_high_ready"), sem("x1_low_ready"), sem("x1_bank_free")
        s_y, s_yA = sem("y_filled"), sem("y_emptied_by_act")
        s_chain = sem("chain_steps")
        s_fold = sem("pool_folds")
        s_merge = sem("tile_sums_merged")
        s_diag, s_G, s_Gout = sem("diag_ready"), sem("g_filled"), sem("g_copied")
        s_k2hi, s_k2lo, s_Ghi, s_Glo, s_l2 = [sem(n) for n in (
            "k2hi_ready", "k2lo_ready", "g_high_ready", "g_low_ready", "l2_done")]
        s_z2s, s_h1, s_h1s, s_h2, s_h2s, s_yy, s_ys, s_out = [sem(n) for n in (
            "z2_ready", "h1_filled", "h1_ready", "h2_filled", "h2_ready", "out_filled",
            "out_ready", "stored")]

        block = ctx.enter_context(nc.Block())

        def over_groups(eng, body):
            with eng.Fori(0, BODIES - 1) as u:
                body(u, False)
            body(BODIES - 1, True)

        def steps_at(slot, last, p):
            return [] if last and slot == GPB - 1 else [n for n in prep_steps() if position(n) == p]

        @block.sync
        def _(sp):
            sp.dma_start(idx[:, :, :], ids).then_inc(s_idx, 16)
            sp.dma_start(base[:, :], first_row).then_inc(s_idx, 16)
            sp.dma_start(ident[:, :], ident_in).then_inc(s_const, 16)
            sp.dma_start(mask[:, :], mask_in).then_inc(s_const, 16)
            sp.dma_start(k1raw[:, :, :], k1.rearrange("h (c n) -> h c n", n=BANK)).then_inc(s_k1, 16)
            sp.dma_start(w0a[:, :], k0a).then_inc(s_w0, 16)
            sp.dma_start(w0b[:, :], k0b).then_inc(s_w0, 16)
            sp.dma_start(w3s[:, :], w3).then_inc(s_mlp, 16)
            sp.dma_start(b1s[:, :], b1).then_inc(s_mlp, 16)
            sp.dma_start(b2s[:, :], b2).then_inc(s_mlp, 16)

            def spread(u, slot):
                g, par = u * GPB + slot + 1, (slot + 1) % 2

                def rows(first, step):
                    return bass.AP(scratch.tensor, (par * ROLLS + first) * GROUP,
                                   [[step * GROUP, KC], [GROUP, M], [1, GROUP]])
                sp.wait_ge(s_gather[par], 16 * GF * (GPB // 2 * u + (slot + 1) // 2 + 1))
                for q in range(FQ):
                    sp.dma_start(scratch[par, q * GF:(q + 1) * GF, :].rearrange("f (b d) -> b f d", d=D),
                                 x0g[par][q * GS:(q + 1) * GS, :, :]).then_inc(s_scratch, 16)
                sp.wait_ge(s_scratch, 16 * FQ * (g + 1))
                sp.dma_start(scratch[par, M:ROLLS, :], scratch[par, 0:ROLLS - M, :]).then_inc(s_again, 16)
                sp.wait_ge(s_again, 16 * (g + 1))
                sp.dma_start(A3[par][0:PR, :], rows(0, 0)).then_inc(s_a3, 16)
                for c in range(NC0):
                    n, buf, _ = chunk(u, slot, c)
                    if slot >= 0 or c >= NR:
                        sp.wait_ge(s_l0, n - NR + 1)
                    sp.dma_start(pairs[buf][0:PR, :], rows(KC * c, 1)).then_inc(s_roll[buf], 16)

            spread(0, -1)
            sp.dma_start(k2s[:, :, :], k2.rearrange("h (m o) -> h m o", o=O)).then_inc(s_k2, 16)

            def body(u, last):
                for slot in range(GPB - last):
                    spread(u, slot)
            over_groups(sp, body)

            sp.wait_ge(s_x1free, NG)
            for k in range(3):
                sp.dma_start(w1s[k][:, :], w1[k * P:(k + 1) * P, :]).then_inc(s_mlp, 16)
            sp.dma_start(w1cs[:, :], w1c).then_inc(s_mlp, 16)
            sp.dma_start(ctxs[:, :], ctxT).then_inc(s_mlp, 16)
            sp.wait_ge(s_merge, MERGE * (NTILES + 2))
            sp.dma_start(w2s[:, :, :], w2.rearrange("(c p) n -> p c n", p=P)).then_inc(s_w2, 16)
            sp.wait_ge(s_ys, 1)
            sp.dma_start(out, ys).then_inc(s_out, 16)
            sp.wait_ge(s_out, 16)

        @block.gpsimd
        def _(pool):
            def take_rows(g, buf):
                nc.gpsimd.tensor_tensor(rows_now[buf][:, :], idx[:, g, :], base[:, :], ALU.add).then_inc(s_rows, 1)
                pool.wait_ge(s_rows, g + 1)

            def gather(buf, fields):
                for f in fields:
                    nc.gpsimd.indirect_dma_start(
                        x0g[buf][:, f, :], None, table,
                        bass.IndirectOffsetOnAxis(ap=rows_now[buf][:, f:f + 1], axis=0)).then_inc(s_gather[buf], 16)

            pool.wait_ge(s_idx, 32)
            for g in range(2):
                take_rows(g, g)
                gather(g, range(GF))
            for i in range(2):
                nc.gpsimd.memset(diag[i][:, :, :], 0.0).then_inc(s_dzero, 1)
            pool.wait_ge(s_dzero, 2)
            pool.wait_ge(s_const, 32)
            for i in range(2):
                nc.gpsimd.tensor_copy(diag[i][:, M, :], mask[:, :]).then_inc(s_dones, 1)
            pool.wait_ge(s_dones, 2)
            nc.gpsimd.memset(fold[1][:, :], 0.0).then_inc(s_fold, FOLDS)
            nc.gpsimd.memset(credit[:, 0:1], 0.0).then_inc(s_G, 1)
            nc.gpsimd.memset(credit[:, 1:2], 0.0).then_inc(s_diag, 1)
            def body(u, last):
                for tile in range(GPB * TPG):
                    slot, j = tile // TPG, tile % TPG
                    T = u * (GPB * TPG) + tile
                    gathers = not last or slot < GPB - 2
                    if gathers and j == 0:
                        pool.wait_ge(s_prod, NC0 * (u * GPB + slot + 1))
                        take_rows(u * GPB + slot + 2, slot % 2)
                    pool.wait_ge(s_xtok, u * GPB + slot + 1)
                    pool.wait_ge(s_G, T + 1)
                    nc.gpsimd.tensor_tensor(
                        diag[tile % 2][:, 0:M, :],
                        xtok[slot % 2][:, j, :].unsqueeze(2).to_broadcast([P, M, SB]),
                        mask[:, :].unsqueeze(1).to_broadcast([P, M, SB]), ALU.mult).then_inc(s_diag, 1)
                    sums = fold[tile % 2]
                    pool.wait_ge(s_merge, MERGE * T + 1)
                    for a in range(2, NA - EXTRA):
                        pool.wait_ge(s_yA, NA * (T + 1) + a + 1)
                        if a > 2:
                            pool.wait_ge(s_fold, FOLDS * (T + 1) + a - 2)
                        nc.gpsimd.tensor_tensor(sums[:, :], scaled[:, 1, :] if a == 2 else sums[:, :],
                                                scaled[:, a, :], ALU.add).then_inc(s_fold, 1)
                    if gathers and j < GATHER_TILES:
                        gather(slot % 2, range(-(-GF * j // GATHER_TILES), -(-GF * (j + 1) // GATHER_TILES)))
            over_groups(pool, body)

        @block.scalar
        def _(act):
            def prep(step, u, slot):
                g, par = (u * GPB + slot + 1, (slot + 1) % 2) if slot >= 0 else (0, 0)
                if step == "xtok":
                    act.wait_ge(s_trans, g + 1)
                    if slot >= 0:
                        act.wait_ge(s_chain, STT * (TPG * (g - 1) + 1))
                        act.wait_ge(s_diag, TPG * (g - 1) + 1)
                    nc.scalar.activation(xtok[par][:, :, :], TR[:, 0:TPG * PR].rearrange(
                        "p (j r) -> p j r", r=PR)[:, :, 0:M], ACT.Copy).then_inc(s_xtok, 1)
                elif step[:2] == "ph":
                    c = int(step[2:])
                    _, hi, free = split(u, slot, c)
                    n, buf, _ = chunk(u, slot, c)
                    act.wait_ge(s_prod, n + 1)
                    if free is not None:
                        act.wait_ge(s_l0, free)
                    nc.scalar.activation(pairs_hi[hi][0:PR, :], pairs[buf][0:PR, :], ACT.Copy).then_inc(s_ph, 1)
                elif step == "x1hi":
                    act.wait_ge(s_l0, NC0 * (g + 1))
                    nc.scalar.activation(x1hi[par][:, :], X1[:, :], ACT.Copy).then_inc(s_x1hi, 1)

            def copy_G(T):
                act.wait_ge(s_G, T + 3)
                nc.scalar.activation(
                    G[:, :, bass.ds((T + 1) * SB, SB)],
                    GB[:, 0:MH * SB].rearrange("p (m b) -> p m b", b=SB), ACT.Copy).then_inc(s_Gout, 1)

            act.wait_ge(s_w0sum, 1)
            nc.scalar.activation(w0hi[:, :], w0s[:, 0:NS * O], ACT.Copy).then_inc(s_w0hi, 1)
            act.wait_ge(s_const, 32)
            act.wait_ge(s_k1, 16)
            for c in range(NCH):
                nc.scalar.activation(k1hi[:, c * BANK:(c + 1) * BANK], k1raw[:, c, :], ACT.Copy).then_inc(s_k1hi, 1)
            act.wait_ge(s_szero, 1)
            nc.scalar.activation(credit[:, 2:3], ident[0:1, 0:1], ACT.Copy).then_inc(s_yA, NA)
            nc.scalar.activation(credit[:, 3:4], ident[0:1, 0:1], ACT.Copy).then_inc(s_Gout, 1)
            for step in prep_steps():
                prep(step, 0, -1)

            def body(u, last):
                for slot in range(GPB):
                    for p in range(TPG * NCH):
                        j, c = p // NCH, p % NCH
                        tile = slot * TPG + j
                        T = u * (GPB * TPG) + tile
                        if OWNER[c] == "A":
                            if rank(c) == 1:
                                act.wait_ge(s_chain, STT * T + MB)
                            elif rank(c) <= NA - EXTRA:
                                act.wait_ge(s_fold, FOLDS * T + max(rank(c) - 2, 1))
                            else:
                                act.wait_ge(s_merge, MERGE * (T + 1) + rank(c) - NA + EXTRA)
                            if rank(c) == 1:
                                act.wait_ge(s_xtok, u * GPB + slot + 1)
                            act.wait_ge(s_y, NCH * T + c + 1)
                            for i in range(MB):
                                m = c * MB + i
                                ins = nc.scalar.activation(
                                    scaled[:, rank(c) - 1, i * O:(i + 1) * O],
                                    Y[(NCH * tile + c) % YB][:, i * O:(i + 1) * O], ACT.Copy,
                                    scale=xtok[slot % 2][:, j, m:m + 1])
                            ins.then_inc(s_yA, 1)
                        for step in steps_at(slot, last, p):
                            prep(step, u, slot)
                        if c == G_AT:
                            copy_G(T - 1)
            over_groups(act, body)
            act.wait_ge(s_k2, 16)
            act.wait_ge(s_y, NCH * NTILES)
            for c in range(NCH):
                if c == NCH // 2:
                    copy_G(NTILES - 1)
                nc.scalar.activation(k2hi[:, c * BANK:(c + 1) * BANK], k2s[:, c * MB:(c + 1) * MB, :],
                                     ACT.Copy).then_inc(s_k2hi, 1)
            act.wait_ge(s_Gout, NTILES + 2)
            for m in range(M):
                if m >= len(Ghi):
                    act.wait_ge(s_l2, m - len(Ghi) + 1)
                nc.scalar.activation(Ghi[m % len(Ghi)][:, :], G[:, m, SB:], ACT.Copy).then_inc(s_Ghi, 1)
            act.wait_ge(s_l2, M)
            nc.scalar.activation(z2[:, :], X1[:, :], ACT.Copy).then_inc(s_z2s, 1)
            act.wait_ge(s_mlp, 8 * 16)
            for i in range(H1 // P):
                act.wait_ge(s_h1, i + 1)
                nc.scalar.activation(h1[:, i, :], Y[i][:, :], ACT.Relu, bias=b1s[:, i:i + 1]).then_inc(s_h1s, 1)
            for i in range(H2 // P):
                act.wait_ge(s_h2, i + 1)
                nc.scalar.activation(h2[:, i, :], H[i][:, :], ACT.Relu, bias=b2s[:, i:i + 1]).then_inc(s_h2s, 1)
            act.wait_ge(s_yy, 1)
            nc.scalar.activation(ys, GB[0:1, :], ACT.Copy).then_inc(s_ys, 1)

        @block.vector
        def _(dve):
            def prep(step, u, slot):
                g, par = (u * GPB + slot + 1, (slot + 1) % 2) if slot >= 0 else (0, 0)
                if step[:4] == "prod":
                    _, buf, fills = chunk(u, slot, int(step[4:]))
                    dve.wait_ge(s_a3, 16 * (g + 1))
                    dve.wait_ge(s_roll[buf], 16 * (fills + 1))
                    nc.vector.tensor_tensor(pairs[buf][0:PR, :], pairs[buf][0:PR, :], A3[par][0:PR, :],
                                            ALU.mult).then_inc(s_prod, 1)
                elif step[:2] == "pl":
                    c = int(step[2:])
                    n, hi, _ = split(u, slot, c)
                    _, buf, _ = chunk(u, slot, c)
                    dve.wait_ge(s_ph, n + 1)
                    nc.vector.tensor_tensor(pairs_lo[buf][0:PR, :], pairs[buf][0:PR, :],
                                            pairs_hi[hi][0:PR, :].bitcast(f32), ALU.subtract).then_inc(s_pl, 1)
                elif step == "x1lo":
                    dve.wait_ge(s_x1hi, g + 1)
                    nc.vector.tensor_tensor(x1lo[par][:, :], X1[:, :], x1hi[par][:, :].bitcast(f32),
                                            ALU.subtract).then_inc(s_x1lo, 1)
                elif step == "z0":
                    nc.vector.tensor_reduce(z0[:, bass.ds(g * (GROUP // D), GROUP // D)],
                                            X1[:, :].rearrange("p (b d) -> p b d", d=D), AX.X,
                                            ALU.add).then_inc(s_x1free, 1)

            def merge(T, par, k):
                sums = chain[par]
                if k == 0:
                    dve.wait_ge(s_chain, STT * (T + 2))
                else:
                    dve.wait_ge(s_merge, MERGE * (T + 2) + k)
                if k < EXTRA:
                    dve.wait_ge(s_yA, NA * (T + 2) - EXTRA + k + 1)
                    a, b, to = sums[:, :], scaled[:, NA - EXTRA + k, :], sums[:, :]
                elif k == EXTRA:
                    dve.wait_ge(s_fold, FOLDS * (T + 2))
                    a, b, to = sums[:, :], fold[par][:, :], sums[:, :]
                else:
                    n = BANK >> (k - EXTRA)
                    a, b = sums[:, 0:n], sums[:, n:2 * n]
                    to = sums[:, 0:n] if k < MERGE - 1 else x2[par][:, :]
                nc.vector.tensor_tensor(to, a, b, ALU.add).then_inc(s_merge, 1)

            nc.vector.memset(chain[1][:, :], 0.0).then_inc(s_chain, STT)
            nc.vector.memset(scaled[:, NA - EXTRA:, :], 0.0).then_inc(s_szero, 1)
            nc.vector.memset(credit[:, 4:5], 0.0).then_inc(s_merge, MERGE)
            dve.wait_ge(s_w0, 32)
            nc.vector.tensor_tensor(w0s[:, 0:NS * O], w0a[:, 0:NS * O], w0b[:, 0:NS * O],
                                    ALU.add).then_inc(s_w0sum, 1)
            if NS < NC0:
                nc.vector.tensor_tensor(w0[:, :], w0a[:, NS * O:], w0b[:, NS * O:], ALU.add).then_inc(s_w0sum, 1)
            dve.wait_ge(s_w0hi, 1)
            nc.vector.tensor_tensor(w0lo[:, :], w0s[:, 0:NS * O], w0hi[:, :].bitcast(f32),
                                    ALU.subtract).then_inc(s_w0lo, 1)
            for c in range(NCH):
                dve.wait_ge(s_k1hi, c + 1)
                nc.vector.tensor_tensor(k1lo[:, c * BANK:(c + 1) * BANK], k1raw[:, c, :],
                                        k1hi[:, c * BANK:(c + 1) * BANK].bitcast(f32),
                                        ALU.subtract).then_inc(s_k1lo, 1)
            for step in prep_steps():
                prep(step, 0, -1)

            def body(u, last):
                for slot in range(GPB):
                    for p in range(TPG * NCH):
                        j, c = p // NCH, p % NCH
                        tile = slot * TPG + j
                        T = u * (GPB * TPG) + tile
                        if OWNER[c] == "D":
                            if rank(c) == 1:
                                dve.wait_ge(s_xtok, u * GPB + slot + 1)
                                dve.wait_ge(s_merge, MERGE * (T + 1))
                                dve.wait_ge(s_yA, NA * (T + 1) + 1)
                            dve.wait_ge(s_y, NCH * T + c + 1)
                            for i in range(MB):
                                m, n = c * MB + i, (rank(c) - 1) * MB + i
                                if n >= MB:
                                    dve.wait_ge(s_chain, STT * (T + 1) + n - MB + 1)
                                nc.vector.scalar_tensor_tensor(
                                    out=chain[tile % 2][:, i * O:(i + 1) * O], in0=Y[(NCH * tile + c) % YB][:, i * O:(i + 1) * O],
                                    scalar=xtok[slot % 2][:, j, m:m + 1],
                                    in1=chain[tile % 2][:, i * O:(i + 1) * O] if n >= MB else scaled[:, 0, i * O:(i + 1) * O],
                                    op0=ALU.mult, op1=ALU.add).then_inc(s_chain, 1)
                        for step in steps_at(slot, last, p):
                            prep(step, u, slot)
                        for k in range(MERGE):
                            if c == MERGE_AT[k]:
                                merge(T - 1, (tile - 1) % 2, k)
            over_groups(dve, body)
            for k in range(MERGE):
                merge(NTILES - 1, (NTILES - 1) % 2, k)
            dve.wait_ge(s_merge, MERGE * (NTILES + 2))
            for c in range(NCH):
                dve.wait_ge(s_k2hi, c + 1)
                nc.vector.tensor_tensor(k2lo[:, c * BANK:(c + 1) * BANK],
                                        k2s[:, c * MB:(c + 1) * MB, :].rearrange("p m o -> p (m o)"),
                                        k2hi[:, c * BANK:(c + 1) * BANK].bitcast(f32), ALU.subtract).then_inc(s_k2lo, 1)
            for m in range(M):
                dve.wait_ge(s_Ghi, m + 1)
                if m >= len(Glo):
                    dve.wait_ge(s_l2, m - len(Glo) + 1)
                nc.vector.tensor_tensor(Glo[m % len(Glo)][:, :], G[:, m, SB:], Ghi[m % len(Ghi)][:, :].bitcast(f32),
                                        ALU.subtract).then_inc(s_Glo, 1)

        @block.tensor
        def _(pe):
            def prep(step, u, slot):
                g = u * GPB + slot + 1 if slot >= 0 else 0
                if step == "xtok":
                    pe.wait_ge(s_a3, 16 * (g + 1))
                    if slot >= 0:
                        pe.wait_ge(s_xtok, g)
                    for j in range(TPG):
                        ins = nc.tensor.transpose(TR[:, j * PR:(j + 1) * PR],
                                                  A3[(slot + 1) % 2][0:PR, j * P:(j + 1) * P], ident[0:PR, 0:PR])
                    ins.then_inc(s_trans, 1)
                elif step[:3] == "l0_":
                    c = int(step[3:])
                    n, buf, _ = chunk(u, slot, c)
                    if c == 0 and slot >= 0:
                        pe.wait_ge(s_x1free, g)
                    if c < NS:
                        k, h, _ = split(u, slot, c)
                        pe.wait_ge(s_pl, k + 1)
                        w, hi, lo = slice(c * O, (c + 1) * O), pairs_hi[h][0:PR, :], pairs_lo[buf][0:PR, :]
                        nc.tensor.matmul(X1[:, :], w0hi[:, w], lo, start=(c == 0), stop=False)
                        nc.tensor.matmul(X1[:, :], w0hi[:, w], hi, start=False, stop=False)
                        nc.tensor.matmul(X1[:, :], w0lo[:, w], hi, start=False,
                                         stop=(c == NC0 - 1)).then_inc(s_l0, 1)
                    else:
                        pe.wait_ge(s_prod, n + 1)
                        nc.tensor.matmul(X1[:, :], w0[:, (c - NS) * O:(c - NS + 1) * O], pairs[buf][0:PR, :],
                                         start=False, stop=(c == NC0 - 1)).then_inc(s_l0, 1)

            def make_G(T, buf):
                pe.wait_ge(s_merge, MERGE * (T + 3))
                pe.wait_ge(s_diag, T + 2)
                pe.wait_ge(s_Gout, T + 2)
                nc.tensor.matmul(GB[:, 0:MH * SB], x2[buf][:, :], diag[buf][:, :, :].rearrange(
                    "p m b -> p (m b)"), start=True, stop=True).then_inc(s_G, 1)

            pe.wait_ge(s_const, 32)
            pe.wait_ge(s_w0lo, 1)
            for step in prep_steps():
                prep(step, 0, -1)

            def body(u, last):
                for slot in range(GPB):
                    pe.wait_ge(s_x1lo, u * GPB + slot + 1)
                    if slot == 0:
                        pe.wait_ge(s_k1lo, NCH)
                    hi, lo = x1hi[slot % 2], x1lo[slot % 2]
                    for p in range(TPG * NCH):
                        j, c = p // NCH, p % NCH
                        tile = slot * TPG + j
                        T = u * (GPB * TPG) + tile
                        Tf, cf = (T, c - YB) if c >= YB else (T - 1, c - YB + NCH)
                        if OWNER[cf] == "A":
                            pe.wait_ge(s_yA, NA * (Tf + 1) + rank(cf))
                        else:
                            pe.wait_ge(s_chain, STT * (Tf + 1) + MB * rank(cf))
                        y = Y[(NCH * tile + c) % YB][:, :]
                        tok, cols = slice(j * P, (j + 1) * P), slice(c * BANK, (c + 1) * BANK)
                        nc.tensor.matmul(y, hi[:, tok], k1lo[:, cols], start=True, stop=False)
                        nc.tensor.matmul(y, hi[:, tok], k1hi[:, cols], start=False, stop=False)
                        nc.tensor.matmul(y, lo[:, tok], k1hi[:, cols], start=False, stop=True).then_inc(s_y, 1)
                        for step in steps_at(slot, last, p):
                            prep(step, u, slot)
                        if c == G_AT:
                            make_G(T - 1, (tile - 1) % 2)
            over_groups(pe, body)
            make_G(NTILES - 1, (NTILES - 1) % 2)

            pe.wait_ge(s_mlp, 8 * 16)
            pe.wait_ge(s_chain, STT * (NTILES + 1))
            pe.wait_ge(s_yA, NA * (NTILES + 1))
            pe.wait_ge(s_x1free, NG)
            for i in range(H1 // P):
                o = slice(i * P, (i + 1) * P)
                nc.tensor.matmul(Y[i][:, :], w1s[0][:, o], z0[:, :], start=True, stop=False)
                nc.tensor.matmul(Y[i][:, :], w1cs[:, o], ctxs[:, :], start=False, stop=False)
            pe.wait_ge(s_Gout, NTILES + 2)
            for i in range(H1 // P):
                nc.tensor.matmul(Y[i][:, :], w1s[1][:, i * P:(i + 1) * P], G[:, M, SB:], start=False, stop=False)
            for m in range(M):
                pe.wait_ge(s_k2lo, m // MB + 1)
                pe.wait_ge(s_Glo, m + 1)
                w, hi, lo = slice(m * O, (m + 1) * O), Ghi[m % len(Ghi)][:, :], Glo[m % len(Glo)][:, :]
                nc.tensor.matmul(X1[:, :], k2lo[:, w], hi, start=(m == 0), stop=False)
                nc.tensor.matmul(X1[:, :], k2hi[:, w], hi, start=False, stop=False)
                nc.tensor.matmul(X1[:, :], k2hi[:, w], lo, start=False, stop=(m == M - 1)).then_inc(s_l2, 1)
            pe.wait_ge(s_z2s, 1)
            for i in range(H1 // P):
                nc.tensor.matmul(Y[i][:, :], w1s[2][:, i * P:(i + 1) * P], z2[:, :], start=False,
                                 stop=True).then_inc(s_h1, 1)
            pe.wait_ge(s_w2, 16)
            for k in range(H1 // P):
                pe.wait_ge(s_h1s, k + 1)
                for i in range(H2 // P):
                    ins = nc.tensor.matmul(H[i][:, :], w2s[:, k, i * P:(i + 1) * P], h1[:, k, :],
                                           start=(k == 0), stop=(k == H1 // P - 1))
                    if k == H1 // P - 1:
                        ins.then_inc(s_h2, 1)
            for k in range(H2 // P):
                pe.wait_ge(s_h2s, k + 1)
                ins = nc.tensor.matmul(GB[0:1, :], w3s[:, k:k + 1], h2[:, k, :], start=(k == 0),
                                       stop=(k == H2 // P - 1))
            ins.then_inc(s_yy, 1)


def first_rows(lengths):
    import numpy as np
    first = np.cumsum([0] + lengths[:-1]).astype(np.int32)
    return np.repeat(first.reshape(FQ, 1, GF), GS, axis=1).reshape(P, GF)


def constants():
    import numpy as np
    mask = (np.arange(P)[:, None] // D == np.arange(SB)[None, :]).astype(np.float32)
    return np.eye(P, dtype=np.float32), mask


def kernel(**inputs):
    import numpy as np
    import concourse.bacc as bacc
    from concourse.bass_utils import run_bass_kernel_spmd

    a = {n: np.asarray(v) for n, v in inputs.items()}
    k0 = a["L0_rec_k0"].transpose(1, 2, 0)
    h = np.arange(M)
    k0a = np.zeros((KC, M, NC0, O), np.float32)
    k0b = np.zeros((KC, M, NC0, O), np.float32)
    for k in range(KD):
        k0a[k % KC, :, k // KC] = k0[h, (h + k) % M]
        if 0 < k < KD - 1:
            k0b[k % KC, :, k // KC] = k0[(h + k) % M, h]
    ident, mask = constants()
    arrays = {
        "ids": a["ids"].reshape(NG, GS, FQ, GF).transpose(2, 1, 0, 3).reshape(P, NG, GF),
        "table": np.concatenate([a[f"tbl_{m}"] for m in range(M)]),
        "first_row": first_rows([len(a[f"tbl_{m}"]) for m in range(M)]),
        "k0a": k0a.reshape(PR, NC0 * O), "k0b": k0b.reshape(PR, NC0 * O),
        "k1": a["L0_rec_k1"].transpose(1, 2, 0).reshape(O, M * O),
        "k2": a["L0_rec_k2"].transpose(1, 2, 0).reshape(O, M * O),
        "ctxT": a["dense_ctx"].T,
        "w1": a["W_top1"][:3 * P], "w1c": a["W_top1"][3 * P:], "b1": a["b_top1"].reshape(-1, P).T,
        "w2": a["W_top2"], "b2": a["b_top2"].reshape(-1, P).T, "w3": a["W_top3"].reshape(-1, P).T,
        "ident": ident, "mask": mask,
    }
    arrays = {n: np.ascontiguousarray(v) for n, v in arrays.items()}
    nc = bacc.Bacc("TRN2", target_bir_lowering=False, num_devices=1)
    ap = {n: nc.dram_tensor("in_" + n, v.shape, mybir.dt.from_np(v.dtype), kind="ExternalInput").ap()
          for n, v in arrays.items()}
    out = nc.dram_tensor("out", (1, B), mybir.dt.float32, kind="ExternalOutput").ap()
    scratch = nc.dram_tensor("scratch", (2, ROLLS, GROUP), mybir.dt.float32, kind="Internal").ap()
    build(nc, ap["ids"], ap["first_row"], ap["table"], ap["k0a"], ap["k0b"], ap["k1"], ap["k2"],
          ap["ctxT"], ap["w1"], ap["w1c"], ap["b1"], ap["w2"], ap["b2"], ap["w3"], ap["ident"],
          ap["mask"], scratch, out)
    r = run_bass_kernel_spmd(nc, [{"in_" + n: v for n, v in arrays.items()}], core_ids=[0])
    return r.results[0]["out"].reshape(B, 1)
```
